# Optimizing a Trainium2 kernel written in Bass

```python
import numpy as np
import jax
import jax.numpy as jnp

def _softmax(x, axis=-1):
    return jax.nn.softmax(x, axis=axis)

def _gelu(x):
    return jax.nn.gelu(x, approximate=True)

def _silu(x):
    return jax.nn.silu(x)

def _sigmoid(x):
    return jax.nn.sigmoid(x)

def _layernorm(x, axis=-1, eps=1e-05):
    m = jnp.mean(x, axis=axis, keepdims=True)
    v = jnp.var(x, axis=axis, keepdims=True)
    return (x - m) / jnp.sqrt(v + eps)

def _scatter_add(tgt, idx, src, axis=0):
    return tgt.at[idx].add(src)

def _segment_sum(src, seg, n):
    return jax.ops.segment_sum(src, seg, n)
kernel_name = 'mk_decoder_preln_d1_seqx_r8_ec8666'

def setup_inputs(seed: int=0):
    np.random.seed(seed)
    _w = jnp.asarray

    def _rec_inputs():
        import jax
        import jax.numpy as jnp
        _rk = jax.random.key(seed)
        x = 0.0003765 + 1 * jax.random.normal(jax.random.fold_in(_rk, 1), (16, 128, 256), jnp.float32)
        _lenS = 128 - jax.random.randint(jax.random.fold_in(_rk, 7), (16,), 0, max(1, 128 // 4) + 1, jnp.int32)
        _lenS2 = 128 - jax.random.randint(jax.random.fold_in(_rk, 8), (16,), 0, max(1, 128 // 4) + 1, jnp.int32)
        _ctx_2048P = jax.random.normal(jax.random.fold_in(_rk, 11), (16, 16, 256), jnp.float32)
        _ctx_2048c = jax.random.dirichlet(jax.random.fold_in(_rk, 511), 0.3 * jnp.ones((16,), jnp.float32), (16, 128))
        _ctx_2048t = jnp.einsum('bsk,bkd->bsd', _ctx_2048c, _ctx_2048P)
        _ctx_2048t = _ctx_2048t * jax.lax.rsqrt(jnp.mean(jnp.square(_ctx_2048t)) + 1e-12) * 0.953939
        ctx_2048 = -0.000292821 + 1.00034 * (_ctx_2048t + 0.3 * jax.random.normal(jax.random.fold_in(_rk, 611), (16, 128, 256), jnp.float32))
        return (x, ctx_2048)
    x, ctx_2048 = _rec_inputs()

    def _L0_attn_setup():
        import jax, jax.numpy as jnp
        import numpy as np
        import math
        D_MODEL = 256
        N_HEADS = 16
        Q_PROJ = D_MODEL // 4
        KV_PROJ = D_MODEL // 4
        DH = D_MODEL // N_HEADS
        LN_EPS = 1e-05

        def _layernorm(x, gamma, beta):
            mu = jnp.mean(x, axis=-1, keepdims=True)
            var = jnp.var(x, axis=-1, keepdims=True)
            return (x - mu) * jax.lax.rsqrt(var + LN_EPS) * gamma + beta
        key = jax.random.key(seed)
        ks = jax.random.split(key, 7)
        B, S = (2, 256)
        x = jax.random.normal(ks[0], (B, S, D_MODEL), dtype=jnp.float32)
        W_dq = 0.01 * jax.random.normal(ks[1], (D_MODEL, Q_PROJ), dtype=jnp.float32)
        W_uq = 0.01 * jax.random.normal(ks[2], (Q_PROJ, D_MODEL), dtype=jnp.float32)
        W_dkv = 0.01 * jax.random.normal(ks[3], (D_MODEL, KV_PROJ), dtype=jnp.float32)
        W_ukv = 0.01 * jax.random.normal(ks[4], (KV_PROJ, 2 * D_MODEL), dtype=jnp.float32)
        W_o = 0.01 * jax.random.normal(ks[5], (D_MODEL, D_MODEL), dtype=jnp.float32)
        q_ln_g = jnp.ones((Q_PROJ,), jnp.float32)
        q_ln_b = jnp.zeros((Q_PROJ,), jnp.float32)
        kv_ln_g = jnp.ones((KV_PROJ,), jnp.float32)
        kv_ln_b = jnp.zeros((KV_PROJ,), jnp.float32)
        return {'x': x, 'W_dq': W_dq, 'W_uq': W_uq, 'q_ln_g': q_ln_g, 'q_ln_b': q_ln_b, 'W_dkv': W_dkv, 'W_ukv': W_ukv, 'kv_ln_g': kv_ln_g, 'kv_ln_b': kv_ln_b, 'W_o': W_o}
    _L0_attn_all = _L0_attn_setup()
    _L0_attn_in = {k: v for k, v in _L0_attn_all.items() if k in ('W_dq', 'W_uq', 'q_ln_g', 'q_ln_b', 'W_dkv', 'W_ukv', 'kv_ln_g', 'kv_ln_b', 'W_o')}
    del _L0_attn_all

    def _L0_xattn_setup():
        import jax, jax.numpy as jnp
        import numpy as np
        key = jax.random.key(seed)
        k1, k2, k3, k4, k5 = jax.random.split(key, 5)
        B, D_MODEL, L = (2, 128, 256)
        HEAD_DIM = 8
        H = D_MODEL // HEAD_DIM
        return {'k': jax.random.normal(k1, (B, D_MODEL, L), dtype=jnp.float32), 'v': jax.random.normal(k2, (B, D_MODEL, L), dtype=jnp.float32), 'q': jax.random.normal(k3, (B, D_MODEL, L), dtype=jnp.float32), 'ssm_kernel': jax.random.normal(k4, (H, L), dtype=jnp.float32), 'D': jax.random.normal(k5, (H,), dtype=jnp.float32), 'head_dim': HEAD_DIM}
    _L0_xattn_all = _L0_xattn_setup()
    _L0_xattn_in = {k: v for k, v in _L0_xattn_all.items() if k in ('ssm_kernel', 'D')}
    del _L0_xattn_all

    def _L0_ffn_setup():
        import jax, jax.numpy as jnp
        import numpy as np
        from jax import lax
        H = 256
        I = 176
        E = 16
        TOP_K = 6
        IS = 2 * I

        def _swiglu(x, w13_, w2_):
            gu = x @ w13_.T
            g, u = jnp.split(gu, 2, axis=-1)
            return jax.nn.silu(g) * u @ w2_.T
        key = jax.random.key(seed)
        ks = jax.random.split(key, 6)
        return {'hidden_states': jax.random.normal(ks[0], (1, 256, H), jnp.float32), 'gate_w': jax.random.normal(ks[1], (E, H), jnp.float32) * 0.02, 'w13': jax.random.normal(ks[2], (E, 2 * I, H), jnp.float32) * 0.02, 'w2': jax.random.normal(ks[3], (E, H, I), jnp.float32) * 0.02, 'sw13': jax.random.normal(ks[4], (2 * IS, H), jnp.float32) * 0.02, 'sw2': jax.random.normal(ks[5], (H, IS), jnp.float32) * 0.02}
    _L0_ffn_all = _L0_ffn_setup()
    _L0_ffn_in = {k: v for k, v in _L0_ffn_all.items() if k in ('gate_w', 'w13', 'w2', 'sw13', 'sw2')}
    del _L0_ffn_all
    return {'x': x, 'ctx_2048': ctx_2048, 'L0_attn_W_dq': _L0_attn_in['W_dq'], 'L0_attn_W_uq': _L0_attn_in['W_uq'], 'L0_attn_q_ln_g': _L0_attn_in['q_ln_g'], 'L0_attn_q_ln_b': _L0_attn_in['q_ln_b'], 'L0_attn_W_dkv': _L0_attn_in['W_dkv'], 'L0_attn_W_ukv': _L0_attn_in['W_ukv'], 'L0_attn_kv_ln_g': _L0_attn_in['kv_ln_g'], 'L0_attn_kv_ln_b': _L0_attn_in['kv_ln_b'], 'L0_attn_W_o': _L0_attn_in['W_o'], 'L0_xattn_ssm_kernel': _L0_xattn_in['ssm_kernel'], 'L0_xattn_D': _L0_xattn_in['D'], 'L0_ffn_gate_w': _L0_ffn_in['gate_w'], 'L0_ffn_w13': _L0_ffn_in['w13'], 'L0_ffn_w2': _L0_ffn_in['w2'], 'L0_ffn_sw13': _L0_ffn_in['sw13'], 'L0_ffn_sw2': _L0_ffn_in['sw2']}

def reference(x, ctx_2048, L0_attn_W_dq, L0_attn_W_uq, L0_attn_q_ln_g, L0_attn_q_ln_b, L0_attn_W_dkv, L0_attn_W_ukv, L0_attn_kv_ln_g, L0_attn_kv_ln_b, L0_attn_W_o, L0_xattn_ssm_kernel, L0_xattn_D, L0_ffn_gate_w, L0_ffn_w13, L0_ffn_w2, L0_ffn_sw13, L0_ffn_sw2):
    import jax
    import jax.numpy as jnp

    def _L0_attn_ref(x, W_dq, W_uq, q_ln_g, q_ln_b, W_dkv, W_ukv, kv_ln_g, kv_ln_b, W_o):
        import jax, jax.numpy as jnp
        import numpy as np
        import math
        D_MODEL = 256
        N_HEADS = 16
        Q_PROJ = D_MODEL // 4
        KV_PROJ = D_MODEL // 4
        DH = D_MODEL // N_HEADS
        LN_EPS = 1e-05

        def _layernorm(x, gamma, beta):
            mu = jnp.mean(x, axis=-1, keepdims=True)
            var = jnp.var(x, axis=-1, keepdims=True)
            return (x - mu) * jax.lax.rsqrt(var + LN_EPS) * gamma + beta
        B, S, D = x.shape
        H, dh = (N_HEADS, DH)
        cq = _layernorm(x @ W_dq, q_ln_g, q_ln_b)
        Q = cq @ W_uq
        ckv = _layernorm(x @ W_dkv, kv_ln_g, kv_ln_b)
        KV = ckv @ W_ukv
        K, V = (KV[..., :D], KV[..., D:])
        q = Q.reshape(B, S, H, dh).transpose(0, 2, 1, 3)
        k = K.reshape(B, S, H, dh).transpose(0, 2, 1, 3)
        v = V.reshape(B, S, H, dh).transpose(0, 2, 1, 3)
        scores = jnp.einsum('bhqd,bhkd->bhqk', q, k) / math.sqrt(float(dh))
        causal = jnp.tril(jnp.ones((S, S), dtype=bool))
        scores = jnp.where(causal, scores, -jnp.inf)
        attn = jax.nn.softmax(scores, axis=-1)
        o = jnp.einsum('bhqk,bhkd->bhqd', attn, v)
        o = o.transpose(0, 2, 1, 3).reshape(B, S, D)
        return o @ W_o.T

    def _L0_xattn_ref(k, v, q, ssm_kernel, D, head_dim):
        import jax, jax.numpy as jnp
        import numpy as np
        B, HD, L = k.shape
        H = HD // head_dim
        fft_size = 2 * L
        k_ = k.reshape(B, H, head_dim, L)
        v_ = v.reshape(B, H, head_dim, L)
        q_ = q.reshape(B, H, head_dim, L)
        kv = jnp.einsum('bhil,bhjl->bijhl', k_, v_)
        kv_f = jnp.fft.rfft(kv, n=fft_size)
        kernel_f = jnp.fft.rfft(ssm_kernel, n=fft_size)
        y = jnp.fft.irfft(kv_f * kernel_f, n=fft_size)[..., :L]
        out = y + kv * D[None, None, None, :, None]
        out = jnp.einsum('bijhl,bhil->bjhl', out, q_)
        out = jnp.transpose(out, (0, 2, 1, 3)).reshape(B, H * head_dim, L)
        return out.astype(k.dtype)

    def _L0_ffn_ref(hidden_states, gate_w, w13, w2, sw13, sw2):
        import jax, jax.numpy as jnp
        import numpy as np
        from jax import lax
        H = 256
        I = 176
        E = 16
        TOP_K = 6
        IS = 2 * I

        def _swiglu(x, w13_, w2_):
            gu = x @ w13_.T
            g, u = jnp.split(gu, 2, axis=-1)
            return jax.nn.silu(g) * u @ w2_.T
        B, S, Hd = hidden_states.shape
        x = hidden_states.reshape(-1, Hd)
        T = x.shape[0]
        scores = jax.nn.softmax(x @ gate_w.T, axis=-1)
        topk_w, topk_ids = lax.top_k(scores, TOP_K)
        topk_w = topk_w / (topk_w.sum(-1, keepdims=True) + 1e-20)
        combine = jnp.einsum('tk,tke->te', topk_w, jax.nn.one_hot(topk_ids, E, dtype=topk_w.dtype))

        def body(acc, ew):
            w13_e, w2_e, c_e = ew
            y = _swiglu(x, w13_e, w2_e)
            return (acc + c_e[:, None] * y, None)
        out, _ = lax.scan(body, jnp.zeros_like(x), (w13, w2, combine.T))
        out = out + _swiglu(x, sw13, sw2)
        return out.reshape(B, S, Hd)
    x = x + _L0_attn_ref(_layernorm(x, axis=-1), L0_attn_W_dq, L0_attn_W_uq, L0_attn_q_ln_g, L0_attn_q_ln_b, L0_attn_W_dkv, L0_attn_W_ukv, L0_attn_kv_ln_g, L0_attn_kv_ln_b, L0_attn_W_o)
    x = x + _L0_xattn_ref(ctx_2048, ctx_2048, _layernorm(x, axis=-1), L0_xattn_ssm_kernel, L0_xattn_D, 8)
    x = x + _L0_ffn_ref(_layernorm(x, axis=-1), L0_ffn_gate_w, L0_ffn_w13, L0_ffn_w2, L0_ffn_sw13, L0_ffn_sw2)
    return x

_drawn_inputs = setup_inputs


def setup_inputs(seed=0):
    import zlib

    import numpy as np

    out = dict(_drawn_inputs(seed))
    spreads = {'L0_attn_q_ln_g': (1.0, 0.6),
     'L0_attn_q_ln_b': (0.0, 0.8),
     'L0_attn_kv_ln_g': (1.0, 0.6),
     'L0_attn_kv_ln_b': (0.0, 0.8)}
    factors = {'L0_attn_W_dq': 8.0,
     'L0_attn_W_uq': 8.0,
     'L0_attn_W_dkv': 8.0,
     'L0_attn_W_ukv': 8.0,
     'L0_attn_W_o': 8.0,
     'L0_ffn_gate_w': 8.0,
     'L0_ffn_w13': 8.0,
     'L0_ffn_w2': 8.0,
     'L0_ffn_sw13': 8.0,
     'L0_ffn_sw2': 8.0}
    for name, (base, spread) in spreads.items():
        noise = np.random.default_rng([zlib.crc32(name.encode()), seed]).standard_normal(out[name].shape)
        drawn = base * np.exp(spread * noise) if base else spread * noise
        out[name] = jnp.asarray(drawn.astype(out[name].dtype))
    for name, factor in factors.items():
        out[name] = (out[name] * factor).astype(out[name].dtype)
    return out
```

```python
from contextlib import ExitStack

import concourse.bass as bass
from concourse import mybir

F32 = mybir.dt.float32
F32R = mybir.dt.float32r
BF16 = mybir.dt.bfloat16
ALU = mybir.AluOpType
ACT = mybir.ActivationFunctionType
AX_X = mybir.AxisListType.X

P = 128
B, S, D = 16, 128, 256
DC = D // P
LAT = 64
H, DH = 16, 16
HS, HD = 16, 8
E, I = 16, 176
TOP = 6
NS = 2
NE = E + NS
UC = 2 * I
NW_UP = DC * NE * UC
HCOLS = NE * I
NCH = -(-HCOLS // P)
LAST = HCOLS - (NCH - 1) * P
NW_DN = NCH * D
SL_UP, SL_DN = NW_UP // B, NW_DN // B
NG = -(-NCH // 4)
EPS = 1e-5
MASKED = -1e30
SCRATCH = 7608
PAIRS = HD * HD

TURN_AT = {0: 5, 1: 8, 2: 11, 3: 14, 4: 16}
DOWN_AT = {0: 7, 1: 10, 2: 13, 3: 16}
TAIL_TURN_AT = {5: 1, 6: 3}
TAIL_DOWN_AT = {4: 0, 5: 3, 6: 5}
CONV_AT = {0: 4, 1: 6, 2: 7, 3: 9}
MIX_AT = {0: 6, 1: 7, 2: 9, 3: 10}


class Tile:

    def __init__(self, n, p, half):
        self.n, self.p, self.half = n, p, half


def fixed(n):
    return Tile(n, n % 2, n // 2)


def looped(k, off):
    return Tile(k * 2 + off, off % 2, k + off // 2)


def later(t):
    return Tile(t.n + 1, 1 - t.p, t.half + t.p)


def wait(eng, sem, value):
    if not isinstance(value, int) or value > 0:
        eng.wait_ge(sem, value)


class Chain:

    def __init__(self, eng, sem, per, n):
        self.eng, self.sem, self.base, self.per, self.k = eng, sem, n * per, per, 0

    def link(self, ins):
        ins.then_inc(self.sem, 1)
        self.k += 1
        self.eng.wait_ge(self.sem, self.base + self.k)

    def close(self):
        assert self.k == self.per, (self.k, self.per)


def build(nc, x, ctx_t, lat_down, lat_gb, lat_up, w_o, toep, gate_w, w_up, w_dn, out):
    x2_dram = nc.dram_tensor("x2_scratch", (B * S, D), F32).ap()
    x2_heads = x2_dram.rearrange("(b h i) d -> h b i d", b=B, h=HS)
    out_heads = out.rearrange("b (h i) d -> h b i d", h=HS)

    with ExitStack() as ctx:
        def sb(name, shape, dt=F32):
            return ctx.enter_context(nc.sbuf_tensor(name, shape, dt))

        def bank(name):
            return ctx.enter_context(nc.psum_tensor(name, [P, 512], F32))

        def sem(name):
            return ctx.enter_context(nc.semaphore(name))

        wu_hi = sb("wu_hi", [P, NW_UP], F32R)
        wu_lo = sb("wu_lo", [P, NW_UP], F32R)
        wd_hi = sb("wd_hi", [P, NW_DN], F32R)
        wd_lo = sb("wd_lo", [P, NW_DN], F32R)
        gw_hi = sb("gw_hi", [P, DC * E], F32R)
        gw_lo = sb("gw_lo", [P, DC * E], F32R)
        ident = sb("ident", [P, P])
        ident_b = sb("ident_b", [P, P], BF16)
        causal = sb("causal", [P, 4 * P], BF16)
        half_neg = sb("half_neg", [P, 2])
        eps = sb("eps", [P, 2])
        gb = sb("gb", [P, 2])
        hT_hi = sb("hT_hi", [P, 4, P], F32R)
        hT_lo = sb("hT_lo", [P, 4, P], F32R)
        kv_hi = sb("kv_hi", [P, DC, B * PAIRS], F32R)
        kv_lo = sb("kv_lo", [P, DC, B * PAIRS], F32R)
        t_hi = sb("t_hi", [P, 2 * P], F32R)
        t_lo = sb("t_lo", [P, 2 * P], F32R)
        xT_hi = sb("xT_hi", [P, 2, DC, P], F32R)
        xT_lo = sb("xT_lo", [P, 2, DC, P], F32R)
        st = sb("st", [P, 2, 6])
        mv = sb("mv", [P, 2])
        ve = sb("ve", [P, 2])
        rstd = sb("rstd", [P, 2])
        mv2 = sb("mv2", [P, 2, 2])
        rstd2 = sb("rstd2", [P, 2])
        nmax = sb("nmax", [P, H])
        rden = sb("rden", [P, H])
        held = sb("held", [P, 1])
        g_max = sb("g_max", [P, 1])
        g_sum = sb("g_sum", [P, 2])
        g_exp = sb("g_exp", [P, E])
        g_score = sb("g_score", [P, E + 8 - TOP])
        g_rest = sb("g_rest", [P, E + 8 - TOP])
        g_top = sb("g_top", [P, 8])
        g_sel = sb("g_sel", [P, E])
        comb = sb("comb", [P, 2, NE])

        scratch = sb("scratch", [P, SCRATCH])
        at = {"a": 0, "b": 0}

        def carve(stage, cols):
            first = at[stage]
            at[stage] += cols
            assert at[stage] <= SCRATCH
            return scratch[:, first:first + cols]

        probs = carve("a", 2 * 4 * P)
        probsT = carve("a", 2 * 4 * P)
        stage_up = carve("a", SL_UP)
        stage_dn = carve("a", SL_DN)
        x_in = carve("a", D)
        x_res = carve("a", D)
        xn = carve("a", D)
        xnT = carve("a", D)
        lat_n = carve("a", 2 * LAT)
        latT = carve("a", P)
        qT = carve("a", DC * P)
        kT = carve("a", 2 * DC * P)
        vals = carve("a", H * (DH + 1)).rearrange("p (h c) -> p h c", h=H)
        att = carve("a", D)
        attT = carve("a", D)
        gw = attT[:, 0:DC * E]
        w_lat = carve("a", DC * 2 * LAT)
        w_latup = carve("a", 3 * D)
        w_out = carve("a", DC * D)

        kv = carve("b", B * PAIRS)
        hid = carve("b", HCOLS)
        mixed = carve("b", 512)
        sil = carve("b", 3 * I)
        xq = carve("b", D)
        xqT = carve("b", D)
        x2_in = carve("b", D)
        ctx_in = carve("b", D)
        toep_in = carve("b", 2 * P + 1)
        conv_o = carve("b", D)
        x3 = [carve("b", D) for _ in range(2)]
        x3n = carve("b", D)

        banks = [bank(f"bank{i}") for i in range(8)]
        score_b = banks[0:4]
        front_b, qv_b, pv_b, proj_b = banks[4:8]
        up_b = banks[0:3]
        turn_b = banks[3]
        down_b = banks[4]
        conv_b = banks[5:7]
        misc_b = banks[7]

        consts_loaded = sem("consts_loaded")
        consts_made = sem("consts_made")
        gw_split = sem("gw_split")
        x_loaded = sem("x_loaded")
        xres_loaded = sem("xres_loaded")
        stage_loaded = sem("stage_loaded")
        weights_split = sem("weights_split")
        x_stats = sem("x_stats")
        x_rstd = sem("x_rstd")
        x_normed = sem("x_normed")
        xn_turned = sem("xn_turned")
        xnT_ready = sem("xnT_ready")
        lat_done = sem("lat_done")
        lat_stats = sem("lat_stats")
        lat_rstd = sem("lat_rstd")
        lat_normed = sem("lat_normed")
        lat_turned = sem("lat_turned")
        latT_ready = sem("latT_ready")
        k_done = sem("k_done")
        v_done = sem("v_done")
        qv_done = sem("qv_done")
        q_taken = sem("q_taken")
        k_taken = sem("k_taken")
        v_taken = sem("v_taken")
        scores_done = sem("scores_done")
        row_max = sem("row_max")
        exp_done = sem("exp_done")
        p_turned = sem("p_turned")
        pT_taken_v = sem("pT_taken_v")
        pT_taken_s = sem("pT_taken_s")
        weighed = sem("weighed")
        att_normed = sem("att_normed")
        att_turned = sem("att_turned")
        attT_ready = sem("attT_ready")
        proj_done = sem("proj_done")
        x2_made = sem("x2_made")
        x2_stored = sem("x2_stored")
        attn_vec = sem("attn_vec")
        attn_pool = sem("attn_pool")

        x2_loaded = sem("x2_loaded")
        ctx_loaded = sem("ctx_loaded")
        toep_loaded = sem("toep_loaded")
        q_stats = sem("q_stats")
        q_rstd = sem("q_rstd")
        q_normed = sem("q_normed")
        q_turned = sem("q_turned")
        qT_ready = sem("qT_ready")
        kv_made = sem("kv_made")
        kv_hi_ready = sem("kv_hi_ready")
        kv_lo_ready = sem("kv_lo_ready")
        toep_made = sem("toep_made")
        toep_hi_ready = sem("toep_hi_ready")
        toep_lo_ready = sem("toep_lo_ready")
        conv_done = sem("conv_done")
        conv_taken = sem("conv_taken")
        conv_mixed = sem("conv_mixed")
        conv_turned = sem("conv_turned")
        x3_made = sem("x3_made")
        x3_stats = sem("x3_stats")
        x3_rstd = sem("x3_rstd")
        x3_normed = sem("x3_normed")
        x3_turned = sem("x3_turned")
        xT_hi_ready = sem("xT_hi_ready")
        xT_lo_ready = sem("xT_lo_ready")
        gate_done = sem("gate_done")
        gate_max = sem("gate_max")
        gate_exp = sem("gate_exp")
        up_done = sem("up_done")
        silu_done = sem("silu_done")
        h_made = sem("h_made")
        h_turned = sem("h_turned")
        hT_hi_ready = sem("hT_hi_ready")
        hT_lo_ready = sem("hT_lo_ready")
        down_read = sem("down_read")
        out_made = sem("out_made")
        out_stored = sem("out_stored")
        front_vec = sem("front_vec")
        front_pool = sem("front_pool")

        ATTN_CONSTS = 6
        FRONT_LINKS = 14

        def hold(value):
            if not isinstance(value, int):
                nc.vector.memset(held[:, :], 0.0)

        block = ctx.enter_context(nc.Block())

        def all_tiles(eng, tile):
            tile(fixed(0), None, fixed(1), fixed(2))
            with eng.Fori(0, (HS - 4) // 2) as k:
                for o in (1, 2):
                    tile(looped(k, o), looped(k, o - 1), looped(k, o + 1), looped(k, o + 2))
            tile(fixed(HS - 3), fixed(HS - 4), fixed(HS - 2), fixed(HS - 1))
            tile(fixed(HS - 2), fixed(HS - 3), fixed(HS - 1), None)
            tile(fixed(HS - 1), fixed(HS - 2), None, None)

        @block.sync
        def _(sp):
            def load_x(b):
                wait(sp, x_normed, b)
                sp.dma_start(x_in, x[b]).then_inc(x_loaded, 16)

            def load_stage(b):
                wait(sp, weights_split, b * 4)
                sp.dma_start(stage_up, w_up[:, bass.ds(b * SL_UP, SL_UP)]).then_inc(stage_loaded, 16)
                sp.dma_start(stage_dn, w_dn[:, bass.ds(b * SL_DN, SL_DN)]).then_inc(stage_loaded, 16)

            def load_res(b):
                wait(sp, x2_stored, b * 16)
                sp.dma_start(x_res, x[b]).then_inc(xres_loaded, 16)

            def store_x2(b):
                sp.wait_ge(x2_made, b + 1)
                sp.dma_start(x2_dram[bass.ds(b * S, S), :], x_res).then_inc(x2_stored, 16)

            load_x(0)
            sp.dma_start(w_lat, lat_down).then_inc(consts_loaded, 16)
            sp.dma_start(gb[:, :], lat_gb).then_inc(consts_loaded, 16)
            sp.dma_start(w_latup, lat_up).then_inc(consts_loaded, 16)
            sp.dma_start(w_out, w_o).then_inc(consts_loaded, 16)
            sp.dma_start(gw, gate_w).then_inc(consts_loaded, 16)
            load_stage(0)
            load_x(1)
            def batch(b):
                load_res(b)
                load_x(b + 2)
                load_stage(b + 1)
                store_x2(b)

            batch(0)
            with sp.Fori(1, B - 2) as b:
                batch(b)
            load_res(B - 2)
            load_stage(B - 1)
            store_x2(B - 2)
            load_res(B - 1)
            store_x2(B - 1)

            sp.wait_ge(x2_stored, 16 * B)
            sp.wait_ge(weights_split, 4 * B)

            def load_x2(t):
                wait(sp, x3_made, t.n)
                sp.dma_start(x2_in, x2_heads[t.n]).then_inc(x2_loaded, 16)

            def load_toep(t):
                wait(sp, toep_lo_ready, t.n)
                sp.dma_start(toep_in, toep[t.n]).then_inc(toep_loaded, 16)

            def load_ctx(t):
                wait(sp, kv_made, t.n * 2)
                sp.dma_start(ctx_in, ctx_t[t.n]).then_inc(ctx_loaded, 16)

            def store_out(t):
                sp.wait_ge(out_made, t.n + 1)
                sp.dma_start(out_heads[t.n], x3[t.p]).then_inc(out_stored, 16)

            def tile(t, prev, nxt, after):
                if after:
                    load_toep(after)
                if prev:
                    store_out(prev)
                if after:
                    load_x2(after)
                    if not (isinstance(after.n, int) and after.n == HS - 1):
                        load_ctx(later(after))

            load_x2(fixed(0))
            load_toep(fixed(0))
            load_ctx(fixed(0))
            load_toep(fixed(1))
            load_x2(fixed(1))
            load_ctx(fixed(1))
            load_ctx(fixed(2))
            all_tiles(sp, tile)
            store_out(fixed(HS - 1))
            sp.wait_ge(out_stored, 16 * HS)

        @block.gpsimd
        def _(pool):
            g = nc.gpsimd
            g.memset(half_neg[:, :], -0.5).then_inc(attn_pool, 1)
            g.memset(eps[:, :], EPS).then_inc(attn_pool, 1)
            g.memset(ident[:, :], 0.0).then_inc(attn_pool, 1)
            g.memset(ident_b[:, :], 0.0).then_inc(attn_pool, 1)
            g.memset(causal[:, :], 0.0).then_inc(attn_pool, 1)
            g.memset(comb[:, :, E:NE], 1.0).then_inc(attn_pool, 1)
            g.memset(g_score[:, E:], -1.0).then_inc(attn_pool, 1)
            g.memset(vals[:, :, DH:DH + 1], 1.0).then_inc(attn_pool, 1)
            pool.wait_ge(attn_pool, 8)
            g.affine_select(out=ident[:, :], in_=ident[:, :], compare_op=ALU.not_equal, fill=1.0, base=0,
                            pattern=[[-1, P]], channel_multiplier=1).then_inc(consts_made, 1)
            g.affine_select(out=ident_b[:, :], in_=ident_b[:, :], compare_op=ALU.not_equal, fill=1.0, base=0,
                            pattern=[[-1, P]], channel_multiplier=1).then_inc(consts_made, 1)
            g.affine_select(out=causal[:, :].rearrange("p (h k) -> p h k", h=4),
                            in_=causal[:, :].rearrange("p (h k) -> p h k", h=4), compare_op=ALU.is_ge,
                            fill=MASKED, base=0, pattern=[[0, 4], [-1, P]],
                            channel_multiplier=1).then_inc(consts_made, 1)
            pool.wait_ge(consts_loaded, 16 * 5)
            g.tensor_copy(gw_hi[:, :], gw).then_inc(gw_split, 1)
            pool.wait_ge(gw_split, 1)
            g.tensor_tensor(gw_lo[:, :], gw, gw_hi[:, :].bitcast(F32), ALU.subtract).then_inc(gw_split, 1)

            def rstd_x(b, k):
                pool.wait_ge(x_stats, b + 1)
                g.tensor_tensor(ve[:, 0:1], mv[:, 1:2], eps[:, 0:1], ALU.add).then_inc(attn_pool, 1)
                pool.wait_ge(attn_pool, k + 1)
                g.tensor_tensor(rstd[:, 0:1], ve[:, 0:1], half_neg[:, 0:1], ALU.pow).then_inc(x_rstd, 1)

            def rstd_lat(b, k):
                pool.wait_ge(x_rstd, b + 1)
                pool.wait_ge(lat_stats, b + 1)
                g.tensor_tensor(ve[:, :], mv2[:, :, 1], eps[:, :], ALU.add).then_inc(attn_pool, 1)
                pool.wait_ge(attn_pool, k + 2)
                g.tensor_tensor(rstd2[:, :], ve[:, :], half_neg[:, :], ALU.pow).then_inc(lat_rstd, 1)

            def split_up(b):
                pool.wait_ge(stage_loaded, b * 32 + 32)
                up = bass.ds(b * SL_UP, SL_UP)
                g.tensor_copy(wu_hi[:, up], stage_up).then_inc(weights_split, 1)
                pool.wait_ge(weights_split, b * 4 + 1)
                g.tensor_tensor(wu_lo[:, up], stage_up, wu_hi[:, up].bitcast(F32),
                                ALU.subtract).then_inc(weights_split, 1)

            def split_dn(b):
                dn = bass.ds(b * SL_DN, SL_DN)
                g.tensor_copy(wd_hi[:, dn], stage_dn).then_inc(weights_split, 1)
                pool.wait_ge(weights_split, b * 4 + 3)
                g.tensor_tensor(wd_lo[:, dn], stage_dn, wd_hi[:, dn].bitcast(F32),
                                ALU.subtract).then_inc(weights_split, 1)

            rstd_x(0, 8)
            rstd_lat(0, 8)
            with pool.Fori(0, B - 1) as b:
                rstd_x(b + 1, b * 2 + 10)
                split_up(b)
                rstd_lat(b + 1, b * 2 + 10)
                split_dn(b)
            split_up(B - 1)
            split_dn(B - 1)

            def rstd_of(t, stats, done, k):
                pool.wait_ge(stats, t.n + 1)
                g.tensor_tensor(ve[:, 0:1], mv[:, 1:2], eps[:, 0:1], ALU.add).then_inc(front_pool, 1)
                pool.wait_ge(front_pool, t.n * 2 + k)
                g.tensor_tensor(rstd[:, 0:1], ve[:, 0:1], half_neg[:, 0:1], ALU.pow).then_inc(done, 1)

            def make_kv(t, lc):
                if lc == 0:
                    pool.wait_ge(ctx_loaded, t.n * 16 + 16)
                c = ctx_in[:, lc * P:(lc + 1) * P].rearrange("p (b i) -> p b i", b=B)
                shape = [P, B, HD, HD]
                wait(pool, kv_lo_ready, t.n * 2 + lc)
                g.tensor_tensor(kv.rearrange("p (b j i) -> p b j i", b=B, j=HD), c.unsqueeze(3).broadcast_to(shape),
                                c.unsqueeze(2).broadcast_to(shape), ALU.mult).then_inc(kv_made, 1)

            def kv_rest(t, lc):
                pool.wait_ge(kv_hi_ready, t.n * 2 + lc + 1)
                g.tensor_tensor(kv_lo[:, lc, :], kv, kv_hi[:, lc, :].bitcast(F32),
                                ALU.subtract).then_inc(kv_lo_ready, 1)

            def tile(t, prev, nxt, after):
                if nxt:
                    rstd_of(nxt, q_stats, q_rstd, 1)
                if after:
                    make_kv(after, 0)
                    kv_rest(after, 0)
                if nxt:
                    rstd_of(nxt, x3_stats, x3_rstd, 2)
                if after:
                    make_kv(after, 1)
                    kv_rest(after, 1)

            rstd_of(fixed(0), q_stats, q_rstd, 1)
            for lc in range(DC):
                make_kv(fixed(0), lc)
                kv_rest(fixed(0), lc)
            make_kv(fixed(1), 0)
            kv_rest(fixed(1), 0)
            rstd_of(fixed(0), x3_stats, x3_rstd, 2)
            make_kv(fixed(1), 1)
            kv_rest(fixed(1), 1)
            all_tiles(pool, tile)

        @block.scalar
        def _(act):
            a = nc.scalar

            def take_xnT(b):
                act.wait_ge(xn_turned, b + 1)
                wait(act, lat_done, b)
                a.copy(xnT, front_b[:, 0:D]).then_inc(xnT_ready, 1)

            def take_latT(b):
                act.wait_ge(lat_turned, b + 1)
                a.activation(latT, front_b[:, 3 * P:4 * P], ACT.Identity, bias=gb[:, 1:2],
                             scale=gb[:, 0:1]).then_inc(latT_ready, 1)

            def take_k(b):
                act.wait_ge(k_done, b + 1)
                wait(act, scores_done, b)
                a.copy(kT, front_b[:, :]).then_inc(k_taken, 1)

            def exps(b, r):
                act.wait_ge(row_max, b * 4 + r + 1)
                wait(act, p_turned, b * 4 + r - 1)
                for s in range(4 * r, 4 * r + 4):
                    ins = a.activation(probs[:, (s % 8) * P:(s % 8 + 1) * P], score_b[r][:, (s % 4) * P:(s % 4 + 1) * P],
                                       ACT.Exp, bias=nmax[:, s:s + 1])
                ins.then_inc(exp_done, 1)

            def batch(b, nxt):
                exps(b, 0)
                if nxt is not None:
                    take_xnT(nxt)
                exps(b, 1)
                exps(b, 2)
                exps(b, 3)
                if nxt is not None:
                    take_latT(nxt)
                act.wait_ge(p_turned, b * 4 + 4)
                act.wait_ge(weighed, b * 4 + 2)
                a.copy(probsT[:, 4 * P:8 * P], score_b[3][:, :]).then_inc(pT_taken_s, 1)
                if nxt is not None:
                    take_k(nxt)
                act.wait_ge(att_turned, b + 1)
                if isinstance(b, int) and b == 0:
                    act.wait_ge(gw_split, 2)
                a.copy(attT, proj_b[:, 0:D]).then_inc(attT_ready, 1)

            act.wait_ge(consts_loaded, 16 * 5)
            take_xnT(0)
            take_latT(0)
            take_k(0)
            batch(0, 1)
            with act.Fori(1, B - 1) as b:
                batch(b, b + 1)
            batch(B - 1, None)

            def kv_round(t, lc):
                act.wait_ge(kv_made, t.n * 2 + lc + 1)
                wait(act, conv_done, t.n * 4)
                a.copy(kv_hi[:, lc, :], kv).then_inc(kv_hi_ready, 1)

            def take_qT(t):
                act.wait_ge(q_turned, t.n + 1)
                wait(act, conv_mixed, t.n * 4)
                a.copy(xqT, misc_b[:, 0:D]).then_inc(qT_ready, 1)

            def toep_round(t):
                act.wait_ge(toep_made, t.n + 1)
                wait(act, conv_done, t.n * 4)
                a.copy(t_hi[:, :], toep_in[:, 0:2 * P]).then_inc(toep_hi_ready, 1)

            def x3T_round(t):
                act.wait_ge(x3_turned, t.n + 1)
                a.copy(xT_hi[:, t.p, :, :], misc_b[:, 0:D].rearrange("p (c n) -> p c n", c=DC)).then_inc(xT_hi_ready, 1)

            def gate_exponent(t):
                act.wait_ge(gate_max, t.n + 1)
                a.activation(g_exp[:, :], misc_b[:, D:D + E], ACT.Exp, bias=g_max[:, 0:1]).then_inc(gate_exp, 1)

            def silu(t, e):
                act.wait_ge(up_done, t.n * NE + e + 1)
                a.activation(sil[:, (e % 3) * I:(e % 3 + 1) * I], up_b[e % 3][:, 0:I], ACT.Silu).then_inc(silu_done, 1)

            def h_round(t, grp):
                act.wait_ge(h_turned, t.n * NG + grp + 1)
                wait(act, down_read, t.n * NG + grp)
                n = min(4, NCH - 4 * grp)
                rows = P if grp < NG - 1 else LAST
                a.copy(hT_hi[0:rows, 0:n, :],
                       turn_b[0:rows, 0:n * P].rearrange("p (c n) -> p c n", c=n)).then_inc(hT_hi_ready, 1)

            def tile(t, prev, nxt, after):
                for e in range(NE):
                    silu(t, e)
                    for grp, s in TAIL_TURN_AT.items():
                        if prev and s == e:
                            h_round(prev, grp)
                    for grp, s in TURN_AT.items():
                        if s == e:
                            h_round(t, grp)
                    if nxt and e == 1:
                        take_qT(nxt)
                    if nxt and e == 2:
                        toep_round(nxt)
                    if after and e == 10:
                        kv_round(after, 0)
                    if after and e == 16:
                        kv_round(after, 1)
                    if nxt and e == 15:
                        x3T_round(nxt)
                    if nxt and e == NE - 1:
                        gate_exponent(nxt)

            take_qT(fixed(0))
            toep_round(fixed(0))
            kv_round(fixed(0), 0)
            kv_round(fixed(0), 1)
            kv_round(fixed(1), 0)
            x3T_round(fixed(0))
            gate_exponent(fixed(0))
            kv_round(fixed(1), 1)
            all_tiles(act, tile)
            h_round(fixed(HS - 1), 5)
            h_round(fixed(HS - 1), 6)

        @block.vector
        def _(dve):
            v = nc.vector

            def vec_links(b):
                return 0 if isinstance(b, int) and b == 0 else b * 3 - 1

            def norm_x(b):
                dve.wait_ge(x_loaded, b * 16 + 16)
                v.bn_stats(st[:, 0, :], x_in).then_inc(attn_vec, 1)
                dve.wait_ge(attn_vec, vec_links(b) + 1)
                hold(b)
                v.bn_aggr(mv[:, :], st[:, 0, :]).then_inc(x_stats, 1)
                dve.wait_ge(x_rstd, b + 1)
                wait(dve, xn_turned, b)
                v.tensor_scalar(xn, x_in, mv[:, 0:1], rstd[:, 0:1], ALU.subtract, ALU.mult).then_inc(x_normed, 1)

            def lat_statistics(b):
                dve.wait_ge(lat_done, b + 1)
                for i in range(2):
                    ins = v.bn_stats(st[:, i, :], front_b[:, 2 * P + i * LAT:2 * P + (i + 1) * LAT])
                ins.then_inc(attn_vec, 1)
                dve.wait_ge(attn_vec, vec_links(b) + 2)
                hold(b)
                for i in range(2):
                    ins = v.bn_aggr(mv2[:, i, :], st[:, i, :])
                ins.then_inc(lat_stats, 1)

            def norm_lat(b):
                dve.wait_ge(lat_rstd, b + 1)
                wait(dve, lat_turned, b)
                for i in range(2):
                    ins = v.tensor_scalar(lat_n[:, i * LAT:(i + 1) * LAT],
                                          front_b[:, 2 * P + i * LAT:2 * P + (i + 1) * LAT],
                                          mv2[:, i, 0:1], rstd2[:, i:i + 1], ALU.subtract, ALU.mult)
                ins.then_inc(lat_normed, 1)

            def take_q(b):
                dve.wait_ge(qv_done, b + 1)
                wait(dve, scores_done, b)
                v.tensor_scalar(qT, qv_b[:, 0:D], float(DH) ** -0.5, None, ALU.mult).then_inc(q_taken, 1)

            def take_v(b):
                wait(dve, weighed, b * 4)
                v.tensor_copy(vals[:, :, 0:DH],
                              qv_b[:, D:2 * D].rearrange("p (h c) -> p h c", h=H)).then_inc(v_taken, 1)

            def take_pT(b, r):
                dve.wait_ge(p_turned, b * 4 + r + 1)
                wait(dve, weighed, b * 4 + r - 1)
                v.tensor_copy(probsT[:, (r % 2) * 4 * P:(r % 2 + 1) * 4 * P], score_b[r][:, :]).then_inc(pT_taken_v, 1)

            def batch(b, nxt):
                if nxt is not None:
                    norm_x(nxt)
                dve.wait_ge(scores_done, b + 1)
                for r in range(4):
                    wait(dve, exp_done, b * 4 + r - 3)
                    v.tensor_reduce(nmax[:, 4 * r:4 * r + 4], score_b[r][:, :].rearrange("p (h k) -> p h k", h=4),
                                    AX_X, ALU.max, negate=True).then_inc(row_max, 1)
                take_pT(b, 0)
                if nxt is not None:
                    lat_statistics(nxt)
                take_pT(b, 1)
                if nxt is not None:
                    norm_lat(nxt)
                take_pT(b, 2)
                if nxt is not None:
                    take_q(nxt)
                dve.wait_ge(weighed, b * 4 + 4)
                o = pv_b[:, 0:H * (DH + 1)].rearrange("p (h c) -> p h c", h=H)
                v.reciprocal(rden[:, :], o[:, :, DH]).then_inc(attn_vec, 1)
                if nxt is not None:
                    take_v(nxt)
                dve.wait_ge(attn_vec, b * 3 + 5 if nxt is not None else b * 3 + 3)
                wait(dve, att_turned, b)
                v.tensor_tensor(att.rearrange("p (h c) -> p h c", h=H), o[:, :, 0:DH],
                                rden[:, :].unsqueeze(2).broadcast_to([P, H, DH]), ALU.mult).then_inc(att_normed, 1)
                dve.wait_ge(proj_done, b + 1)
                dve.wait_ge(xres_loaded, b * 16 + 16)
                v.tensor_tensor(x_res, proj_b[:, D:2 * D], x_res, ALU.add).then_inc(x2_made, 1)

            norm_x(0)
            lat_statistics(0)
            norm_lat(0)
            take_q(0)
            take_v(0)
            batch(0, 1)
            with dve.Fori(1, B - 1) as b:
                batch(b, b + 1)
            batch(B - 1, None)

            def statistics(src, done, chain):
                chain.link(v.bn_stats(st[:, 0, :], src))
                hold(chain.base)
                v.bn_aggr(mv[:, :], st[:, 0, :]).then_inc(done, 1)

            def norm_q(t, chain):
                dve.wait_ge(x2_loaded, t.n * 16 + 16)
                statistics(x2_in, q_stats, chain)
                dve.wait_ge(q_rstd, t.n + 1)
                v.tensor_scalar(xq, x2_in, mv[:, 0:1], rstd[:, 0:1], ALU.subtract, ALU.mult).then_inc(q_normed, 1)

            def toep_diag(t):
                w = toep_in
                dve.wait_ge(toep_loaded, t.n * 16 + 16)
                v.scalar_tensor_tensor(out=w[:, 0:P], in0=ident[:, :], scalar=w[:, 2 * P:2 * P + 1], in1=w[:, 0:P],
                                       op0=ALU.mult, op1=ALU.add).then_inc(toep_made, 1)

            def toep_rest(t):
                dve.wait_ge(toep_hi_ready, t.n + 1)
                v.tensor_tensor(t_lo[:, :], toep_in[:, 0:2 * P], t_hi[:, :].bitcast(F32),
                                ALU.subtract).then_inc(toep_lo_ready, 1)

            def mix(t, u, chain):
                lc, n = divmod(u, 2)
                if u == 0:
                    dve.wait_ge(qT_ready, t.n + 1)
                dve.wait_ge(conv_done, t.n * 4 + u + 1)
                wait(dve, conv_mixed, t.n * 4 + u)
                shape = [P, B // 2, HD, HD]
                m = mixed.rearrange("p (b j i) -> p b j i", b=B // 2, j=HD)
                q = xqT[:, lc * P + n * 64:lc * P + (n + 1) * 64].rearrange("p (b i) -> p b i", b=B // 2)
                v.tensor_tensor(m, conv_b[u % 2][:, :].rearrange("p (b j i) -> p b j i", b=B // 2, j=HD),
                                q.unsqueeze(2).broadcast_to(shape), ALU.mult).then_inc(conv_taken, 1)
                dve.wait_ge(conv_taken, t.n * 4 + u + 1)
                v.tensor_reduce(conv_o[:, lc * P + n * 64:lc * P + (n + 1) * 64],
                                mixed.rearrange("p (o i) -> p o i", i=HD),
                                AX_X, ALU.add).then_inc(conv_mixed, 1)

            def make_x3(t, chain):
                dve.wait_ge(conv_turned, t.n + 1)
                wait(dve, out_stored, t.n * 16 - 16)
                v.tensor_tensor(x3[t.p], misc_b[:, 0:D], x2_in, ALU.add).then_inc(x3_made, 1)
                dve.wait_ge(x3_made, t.n + 1)
                statistics(x3[t.p], x3_stats, chain)

            def norm_x3(t):
                dve.wait_ge(x3_rstd, t.n + 1)
                v.tensor_scalar(x3n, x3[t.p], mv[:, 0:1], rstd[:, 0:1], ALU.subtract, ALU.mult).then_inc(x3_normed, 1)

            def x3T_rest(t):
                dve.wait_ge(xT_hi_ready, t.n + 1)
                v.tensor_tensor(xT_lo[:, t.p, :, :], misc_b[:, 0:D].rearrange("p (c n) -> p c n", c=DC),
                                xT_hi[:, t.p, :, :].bitcast(F32), ALU.subtract).then_inc(xT_lo_ready, 1)

            def gating(t, chain):
                dve.wait_ge(gate_done, t.n + 1)
                v.tensor_reduce(g_max[:, :], misc_b[:, D:D + E], AX_X, ALU.max, negate=True).then_inc(gate_max, 1)
                dve.wait_ge(gate_exp, t.n + 1)
                chain.link(v.reduce_sum(g_sum[:, 0:1], g_exp[:, :], AX_X))
                chain.link(v.reciprocal(g_sum[:, 1:2], g_sum[:, 0:1]))
                chain.link(v.tensor_scalar(g_score[:, 0:E], g_exp[:, :], g_sum[:, 1:2], None, ALU.mult))
                hold(chain.base)
                chain.link(v.max(g_top[:, :], g_score[:, 0:E]))
                chain.link(v.memset(g_top[:, TOP:8], -1.0))
                hold(chain.base)
                chain.link(v.match_replace(g_rest[:, :], g_top[:, :], g_score[:, :], 0.0))
                chain.link(v.tensor_tensor(g_sel[:, :], g_score[:, 0:E], g_rest[:, 0:E], ALU.subtract))
                chain.link(v.reduce_sum(g_sum[:, 0:1], g_sel[:, :], AX_X))
                chain.link(v.tensor_scalar(g_sum[:, 0:1], g_sum[:, 0:1], 1e-20, None, ALU.add))
                chain.link(v.reciprocal(g_sum[:, 1:2], g_sum[:, 0:1]))
                chain.link(v.tensor_scalar(comb[:, t.p, 0:E], g_sel[:, :], g_sum[:, 1:2], None, ALU.mult))

            def hidden(t, e):
                dve.wait_ge(silu_done, t.n * NE + e + 1)
                grp = (I * (e + 1) - 1) // 512
                wait(dve, h_turned, t.n * NG - NG + grp + 1)
                v.scalar_tensor_tensor(out=hid[:, e * I:(e + 1) * I], in0=sil[:, (e % 3) * I:(e % 3 + 1) * I],
                                       scalar=comb[:, t.p, e:e + 1], in1=up_b[e % 3][:, I:2 * I],
                                       op0=ALU.mult, op1=ALU.mult).then_inc(h_made, 1)

            def h_rest(t, grp):
                dve.wait_ge(hT_hi_ready, t.n * NG + grp + 1)
                n = min(4, NCH - 4 * grp)
                rows = P if grp < NG - 1 else LAST
                v.tensor_tensor(hT_lo[0:rows, 0:n, :], turn_b[0:rows, 0:n * P].rearrange("p (c n) -> p c n", c=n),
                                hT_hi[0:rows, 0:n, :].bitcast(F32), ALU.subtract).then_inc(hT_lo_ready, 1)

            def finish(t):
                dve.wait_ge(down_read, t.n * NG + NG)
                v.tensor_tensor(x3[t.p], down_b[:, 0:D], x3[t.p], ALU.add).then_inc(out_made, 1)

            def tile(t, prev, nxt, after):
                chain = Chain(dve, front_vec, FRONT_LINKS - 1, nxt.n) if nxt else None
                if nxt:
                    norm_q(nxt, chain)
                for e in range(NE):
                    hidden(t, e)
                    for grp, s in TAIL_TURN_AT.items():
                        if prev and s == e:
                            h_rest(prev, grp)
                    for grp, s in TURN_AT.items():
                        if s == e:
                            h_rest(t, grp)
                    if nxt and e == 0:
                        toep_diag(nxt)
                    if nxt and e == 2:
                        toep_rest(nxt)
                    if prev and e == 6:
                        finish(prev)
                    for u, s in MIX_AT.items():
                        if nxt and s == e:
                            mix(nxt, u, chain)
                    if nxt and e == 12:
                        make_x3(nxt, chain)
                    if nxt and e == 13:
                        norm_x3(nxt)
                    if nxt and e == 15:
                        x3T_rest(nxt)
                if nxt:
                    gating(nxt, chain)
                    chain.close()

            chain = Chain(dve, front_vec, FRONT_LINKS - 1, 0)
            t0 = fixed(0)
            dve.wait_ge(consts_made, 3)
            norm_q(t0, chain)
            toep_diag(t0)
            toep_rest(t0)
            for u in range(4):
                mix(t0, u, chain)
            make_x3(t0, chain)
            norm_x3(t0)
            x3T_rest(t0)
            gating(t0, chain)
            chain.close()
            all_tiles(dve, tile)
            h_rest(fixed(HS - 1), 5)
            h_rest(fixed(HS - 1), 6)
            finish(fixed(HS - 1))

        @block.tensor
        def _(pe):
            mm = nc.tensor.matmul

            def turn_x(b):
                pe.wait_ge(x_normed, b + 1)
                wait(pe, k_taken, b)
                for c in range(DC):
                    ins = nc.tensor.transpose(front_b[:, c * P:(c + 1) * P], xn[:, c * P:(c + 1) * P], ident[:, :])
                ins.then_inc(xn_turned, 1)

            def latents(b):
                pe.wait_ge(xnT_ready, b + 1)
                for c in range(DC):
                    ins = mm(front_b[:, 2 * P:3 * P], xnT[:, c * P:(c + 1) * P], w_lat[:, c * P:(c + 1) * P],
                             start=(c == 0), stop=(c == DC - 1))
                ins.then_inc(lat_done, 1)

            def turn_lat(b):
                pe.wait_ge(lat_normed, b + 1)
                nc.tensor.transpose(front_b[:, 3 * P:4 * P], lat_n, ident[:, :]).then_inc(lat_turned, 1)

            def keys(b):
                pe.wait_ge(latT_ready, b + 1)
                for v in range(2):
                    for c in range(DC):
                        o = (v * DC + c) * P
                        ins = mm(front_b[:, o:o + P], w_latup[LAT:, D + o:D + o + P], latT[LAT:, :],
                                 start=True, stop=True)
                ins.then_inc(k_done, 1)

            def values(b):
                pe.wait_ge(latT_ready, b + 1)
                wait(pe, q_taken, b)
                wait(pe, v_taken, b)
                mm(qv_b[:, D:2 * D], latT[LAT:2 * LAT, :], w_latup[LAT:2 * LAT, 0:D],
                   start=True, stop=True).then_inc(v_done, 1)

            def queries(b):
                pe.wait_ge(v_done, b + 1)
                for c in range(DC):
                    ins = mm(qv_b[:, c * P:(c + 1) * P], w_latup[0:LAT, c * P:(c + 1) * P], latT[0:LAT, :],
                             start=True, stop=True)
                ins.then_inc(qv_done, 1)

            def scores(b):
                pe.wait_ge(q_taken, b + 1)
                pe.wait_ge(k_taken, b + 1)
                wait(pe, pT_taken_v, b * 3)
                wait(pe, pT_taken_s, b)
                for r in range(4):
                    mm(score_b[r][:, :], ident_b[:, :], causal[:, :], start=True, stop=False, skip_group_check=True)
                for c in range(DC):
                    for v in range(2):
                        for r in range(4):
                            o = (2 * c + v) * P
                            rows = slice(32 * r, 32 * r + 32)
                            ins = mm(score_b[r][:, o:o + P], qT[rows, c * P:(c + 1) * P],
                                     kT[rows, (v * DC + c) * P:(v * DC + c + 1) * P],
                                     start=False, stop=(c == 1 and v == 1), skip_group_check=True)
                ins.then_inc(scores_done, 1)

            def turn_p(b, r):
                pe.wait_ge(exp_done, b * 4 + r + 1)
                for s in range(4):
                    ins = nc.tensor.transpose(score_b[r][:, s * P:(s + 1) * P],
                                              probs[:, (4 * (r % 2) + s) * P:(4 * (r % 2) + s + 1) * P], ident[:, :])
                ins.then_inc(p_turned, 1)

            def weigh(b, r):
                if r == 0:
                    pe.wait_ge(v_taken, b + 1)
                    wait(pe, att_normed, b)
                if r < 3:
                    pe.wait_ge(pT_taken_v, b * 3 + r + 1)
                else:
                    pe.wait_ge(pT_taken_s, b + 1)
                for s in range(4):
                    h = 8 * (s // 2) + 2 * r + s % 2
                    o = h * (DH + 1)
                    q = (4 * (r % 2) + s) * P
                    ins = mm(pv_b[:, o:o + DH + 1], probsT[:, q:q + P], vals[:, h, :], start=True, stop=True)
                ins.then_inc(weighed, 1)

            def project(b):
                pe.wait_ge(att_normed, b + 1)
                wait(pe, x2_made, b)
                for c in range(DC):
                    ins = nc.tensor.transpose(proj_b[:, c * P:(c + 1) * P], att[:, c * P:(c + 1) * P], ident[:, :])
                ins.then_inc(att_turned, 1)
                pe.wait_ge(attT_ready, b + 1)
                for c in range(DC):
                    ins = mm(proj_b[:, D:2 * D], attT[:, c * P:(c + 1) * P], w_out[:, c * D:(c + 1) * D],
                             start=(c == 0), stop=(c == DC - 1))
                ins.then_inc(proj_done, 1)

            def batch(b, nxt):
                more = nxt is not None
                scores(b)
                if more:
                    turn_x(nxt)
                turn_p(b, 0)
                if more:
                    latents(nxt)
                turn_p(b, 1)
                weigh(b, 0)
                turn_p(b, 2)
                if more:
                    turn_lat(nxt)
                weigh(b, 1)
                turn_p(b, 3)
                if more:
                    values(nxt)
                    keys(nxt)
                    queries(nxt)
                weigh(b, 2)
                weigh(b, 3)
                project(b)

            pe.wait_ge(consts_loaded, 16 * 5)
            pe.wait_ge(consts_made, 3)
            turn_x(0)
            latents(0)
            turn_lat(0)
            values(0)
            keys(0)
            queries(0)
            batch(0, 1)
            with pe.Fori(1, B - 1) as b:
                batch(b, b + 1)
            batch(B - 1, None)

            def three(out_ap, stat, mov, first, last):
                (s_hi, s_lo), (m_hi, m_lo) = stat, mov
                mm(out_ap, s_hi, m_hi, start=first, stop=False)
                mm(out_ap, s_hi, m_lo, start=False, stop=False)
                return mm(out_ap, s_lo, m_hi, start=False, stop=last)

            def turn_q(t):
                pe.wait_ge(q_normed, t.n + 1)
                wait(pe, gate_exp, t.n)
                for c in range(DC):
                    ins = nc.tensor.transpose(misc_b[:, c * P:(c + 1) * P], xq[:, c * P:(c + 1) * P], ident[:, :])
                ins.then_inc(q_turned, 1)

            def conv(t, u):
                lc, n = divmod(u, 2)
                if u == 0:
                    pe.wait_ge(toep_lo_ready, t.n + 1)
                    pe.wait_ge(kv_lo_ready, t.n * 2 + 2)
                wait(pe, conv_taken, t.n * 4 + u - 1)
                cols = slice(n * 512, (n + 1) * 512)
                for mc in range(lc + 1):
                    tap = slice((lc - mc) * P, (lc - mc + 1) * P)
                    ins = three(conv_b[u % 2][:, :], (t_hi[:, tap], t_lo[:, tap]),
                                (kv_hi[:, mc, cols], kv_lo[:, mc, cols]), mc == 0, mc == lc)
                ins.then_inc(conv_done, 1)

            def turn_conv(t):
                pe.wait_ge(conv_mixed, t.n * 4 + 4)
                pe.wait_ge(qT_ready, t.n + 1)
                for c in range(DC):
                    ins = nc.tensor.transpose(misc_b[:, c * P:(c + 1) * P], conv_o[:, c * P:(c + 1) * P], ident[:, :])
                ins.then_inc(conv_turned, 1)

            def turn_x3(t):
                pe.wait_ge(x3_normed, t.n + 1)
                for c in range(DC):
                    ins = nc.tensor.transpose(misc_b[:, c * P:(c + 1) * P], x3n[:, c * P:(c + 1) * P], ident[:, :])
                ins.then_inc(x3_turned, 1)

            def gate(t):
                pe.wait_ge(xT_lo_ready, t.n + 1)
                for c in range(DC):
                    ins = three(misc_b[:, D:D + E], (xT_hi[:, t.p, c, :], xT_lo[:, t.p, c, :]),
                                (gw_hi[:, c * E:(c + 1) * E], gw_lo[:, c * E:(c + 1) * E]), c == 0, c == DC - 1)
                ins.then_inc(gate_done, 1)

            def up(t, e):
                if e == 0:
                    pe.wait_ge(xT_lo_ready, t.n + 1)
                wait(pe, h_made, t.n * NE + e - 2)
                for c in range(DC):
                    o = (c * NE + e) * UC
                    ins = three(up_b[e % 3][:, 0:UC], (xT_hi[:, t.p, c, :], xT_lo[:, t.p, c, :]),
                                (wu_hi[:, o:o + UC], wu_lo[:, o:o + UC]), c == 0, c == DC - 1)
                ins.then_inc(up_done, 1)

            def turn_h(t, grp):
                last_expert = (min(512 * (grp + 1), HCOLS) - 1) // I
                pe.wait_ge(h_made, t.n * NE + last_expert + 1)
                wait(pe, hT_lo_ready, t.n * NG + grp)
                for j in range(4 * grp, min(4 * grp + 4, NCH)):
                    rows = P if j < NCH - 1 else LAST
                    ins = nc.tensor.transpose(turn_b[0:rows, (j % 4) * P:(j % 4 + 1) * P], hid[:, j * P:j * P + rows],
                                              ident[:, :])
                ins.then_inc(h_turned, 1)

            def down(t, grp):
                pe.wait_ge(hT_lo_ready, t.n * NG + grp + 1)
                if grp == 0:
                    wait(pe, out_made, t.n)
                for j in range(4 * grp, min(4 * grp + 4, NCH)):
                    rows = P if j < NCH - 1 else LAST
                    ins = three(down_b[:, 0:D], (hT_hi[0:rows, j % 4, :], hT_lo[0:rows, j % 4, :]),
                                (wd_hi[0:rows, j * D:(j + 1) * D], wd_lo[0:rows, j * D:(j + 1) * D]),
                                j == 0, j == NCH - 1)
                ins.then_inc(down_read, 1)

            def tile(t, prev, nxt, after):
                for e in range(NE):
                    up(t, e)
                    for grp, s in TAIL_DOWN_AT.items():
                        if prev and s == e:
                            down(prev, grp)
                    for grp, s in DOWN_AT.items():
                        if s == e:
                            down(t, grp)
                    if nxt and e == 1:
                        turn_q(nxt)
                    for grp, s in TAIL_TURN_AT.items():
                        if prev and s == e:
                            turn_h(prev, grp)
                    for grp, s in TURN_AT.items():
                        if s == e:
                            turn_h(t, grp)
                    for u, s in CONV_AT.items():
                        if nxt and s == e:
                            conv(nxt, u)
                    if nxt and e == 12:
                        turn_conv(nxt)
                    if nxt and e == 15:
                        turn_x3(nxt)
                if nxt:
                    gate(nxt)

            pe.wait_ge(gw_split, 2)
            t0 = fixed(0)
            turn_q(t0)
            for u in range(4):
                conv(t0, u)
            turn_conv(t0)
            turn_x3(t0)
            gate(t0)
            pe.wait_ge(weights_split, 4 * B)
            all_tiles(pe, tile)
            end = fixed(HS - 1)
            down(end, 4)
            turn_h(end, 5)
            down(end, 5)
            turn_h(end, 6)
            down(end, 6)


def kernel(x, ctx_2048, L0_attn_W_dq, L0_attn_W_uq, L0_attn_q_ln_g, L0_attn_q_ln_b, L0_attn_W_dkv, L0_attn_W_ukv,
           L0_attn_kv_ln_g, L0_attn_kv_ln_b, L0_attn_W_o, L0_xattn_ssm_kernel, L0_xattn_D, L0_ffn_gate_w,
           L0_ffn_w13, L0_ffn_w2, L0_ffn_sw13, L0_ffn_sw2):
    import numpy as np
    import concourse.bacc as bacc
    from concourse.bass_utils import run_bass_kernel_spmd

    f = np.float32
    a = {k: np.asarray(w) for k, w in dict(
        x=x, ctx=ctx_2048, wdq=L0_attn_W_dq, wuq=L0_attn_W_uq, qg=L0_attn_q_ln_g, qb=L0_attn_q_ln_b,
        wdkv=L0_attn_W_dkv, wukv=L0_attn_W_ukv, kg=L0_attn_kv_ln_g, kb=L0_attn_kv_ln_b, wo=L0_attn_W_o,
        taps=L0_xattn_ssm_kernel, skip=L0_xattn_D, gate=L0_ffn_gate_w, w13=L0_ffn_w13, w2=L0_ffn_w2,
        sw13=L0_ffn_sw13, sw2=L0_ffn_sw2).items()}

    def chunked(w):
        return np.ascontiguousarray(w.reshape(-1, P, w.shape[1]).transpose(1, 0, 2).reshape(P, -1))

    w_k = np.zeros((LAT, 2, H, DH), f)
    for v in range(2):
        w_k[:, v, v::2] = a["wukv"][:, 0:D].reshape(LAT, H, DH)[:, v::2]
    lat_up = np.zeros((P, 3 * D), f)
    lat_up[0:LAT, 0:D] = a["wuq"]
    lat_up[LAT:, D:] = w_k.reshape(LAT, 2 * D)
    lat_up[LAT:, 0:D] = a["wukv"][:, D:]
    padded = np.concatenate([np.zeros((HS, P - 1), f), a["taps"]], axis=1)
    toep = np.empty((HS, P, 2 * P + 1), f)
    toep[:, :, 0:2 * P] = padded[:, P - 1 - np.arange(P)[:, None] + np.arange(2 * P)[None, :]]
    toep[:, :, 2 * P] = a["skip"][:, None]
    ctx_t = a["ctx"].reshape(B, HS, HD, DC, P).transpose(1, 4, 3, 0, 2).reshape(HS, P, DC * P)
    s13 = a["sw13"].reshape(2, NS, I, D).transpose(1, 0, 2, 3).reshape(NS, UC, D)
    w13 = np.concatenate([a["w13"], s13], axis=0)
    w_up = w13.reshape(NE, UC, DC, P).transpose(3, 2, 0, 1).reshape(P, NW_UP)
    w2 = np.concatenate([a["w2"].transpose(0, 2, 1).reshape(E * I, D), a["sw2"].T,
                         np.zeros((NCH * P - HCOLS, D), f)], axis=0)

    arrays = dict(
        x=a["x"], ctx_t=ctx_t, lat_down=chunked(np.concatenate([a["wdq"], a["wdkv"]], axis=1)),
        lat_gb=np.stack([np.concatenate([a["qg"], a["kg"]]), np.concatenate([a["qb"], a["kb"]])], axis=1),
        lat_up=lat_up, w_o=chunked(a["wo"].T), toep=toep, gate_w=chunked(a["gate"].T), w_up=w_up, w_dn=chunked(w2))
    nc = bacc.Bacc("TRN2", target_bir_lowering=False, num_devices=1)
    arrays = {f"in_{k}": np.ascontiguousarray(w) for k, w in arrays.items()}
    args = [nc.dram_tensor(k, w.shape, F32, kind="ExternalInput").ap() for k, w in arrays.items()]
    out = nc.dram_tensor("out_x", (B, S, D), F32, kind="ExternalOutput").ap()
    build(nc, *args, out)
    r = run_bass_kernel_spmd(nc, [arrays], core_ids=[0])
    return r.results[0]["out_x"]
```

```python
from contextlib import ExitStack

import concourse.bass as bass
from concourse import mybir

F32 = mybir.dt.float32
F32R = mybir.dt.float32r
BF16 = mybir.dt.bfloat16
ALU = mybir.AluOpType
ACT = mybir.ActivationFunctionType
AX_X = mybir.AxisListType.X

P = 128
B, S, D = 16, 128, 256
DC = D // P
LAT = 64
H, DH = 16, 16
HS, HD = 16, 8
E, I = 16, 176
TOP = 6
NS = 2
NE = E + NS
UC = 2 * I
NW_UP = DC * NE * UC
HCOLS = NE * I
NCH = -(-HCOLS // P)
LAST = HCOLS - (NCH - 1) * P
NW_DN = NCH * D
SL_UP, SL_DN = NW_UP // B, NW_DN // B
NG = -(-NCH // 4)
EPS = 1e-5
MASKED = -1e30
SCRATCH = 7608
PAIRS = HD * HD

TURN_AT = {0: 5, 1: 8, 2: 11, 3: 14, 4: 16}
DOWN_AT = {0: 7, 1: 10, 2: 13, 3: 16}
TAIL_TURN_AT = {5: 1, 6: 3}
TAIL_DOWN_AT = {4: 0, 5: 3, 6: 5}
CONV_AT = {0: 1, 1: 2, 2: 4, 3: 6}
MIX_AT = {0: 3, 1: 4, 2: 6, 3: 8}


class Tile:

    def __init__(self, n, p, half):
        self.n, self.p, self.half = n, p, half


def fixed(n):
    return Tile(n, n % 2, n // 2)


def looped(k, off):
    return Tile(k * 2 + off, off % 2, k + off // 2)


def later(t):
    return Tile(t.n + 1, 1 - t.p, t.half + t.p)


def wait(eng, sem, value):
    if not isinstance(value, int) or value > 0:
        eng.wait_ge(sem, value)


class Chain:

    def __init__(self, eng, sem, base):
        self.eng, self.sem, self.base, self.k = eng, sem, base, 0

    def link(self, ins):
        ins.then_inc(self.sem, 1)
        self.k += 1
        self.eng.wait_ge(self.sem, self.base + self.k)

    def close(self, links):
        assert self.k == links, (self.k, links)


def build(nc, x, ctx_t, lat_down, lat_gb, lat_up, w_o, toep, gate_w, w_up, w_dn, out):
    x2_dram = nc.dram_tensor("x2_scratch", (B * S, D), F32).ap()
    x2_heads = x2_dram.rearrange("(b h i) d -> h b i d", b=B, h=HS)
    out_heads = out.rearrange("b (h i) d -> h b i d", h=HS)

    with ExitStack() as ctx:
        def sb(name, shape, dt=F32):
            return ctx.enter_context(nc.sbuf_tensor(name, shape, dt))

        def bank(name):
            return ctx.enter_context(nc.psum_tensor(name, [P, 512], F32))

        def sem(name):
            return ctx.enter_context(nc.semaphore(name))

        wu_hi = sb("wu_hi", [P, NW_UP], F32R)
        wu_lo = sb("wu_lo", [P, NW_UP], F32R)
        wd_hi = sb("wd_hi", [P, NW_DN], F32R)
        wd_lo = sb("wd_lo", [P, NW_DN], F32R)
        gw_hi = sb("gw_hi", [P, DC * E], F32R)
        gw_lo = sb("gw_lo", [P, DC * E], F32R)
        ident = sb("ident", [P, P])
        ident_b = sb("ident_b", [P, P], BF16)
        causal = sb("causal", [P, 4 * P], BF16)
        half_neg = sb("half_neg", [P, 2])
        eps = sb("eps", [P, 2])
        gb = sb("gb", [P, 2])
        with nc.sbuf_tensor("keys_blocks", [P, 4 * 4 * P], F32) as keys_blocks:
            kT = keys_blocks[:, :]
        kv_hi = sb("kv_hi", [P, DC, B * PAIRS], F32R)
        hT_hi = sb("hT_hi", [P, 4, P], F32R)
        hT_lo = sb("hT_lo", [P, 4, P], F32R)
        kv_lo = sb("kv_lo", [P, DC, B * PAIRS], F32R)
        t_hi = sb("t_hi", [P, 2 * P], F32R)
        t_lo = sb("t_lo", [P, 2 * P], F32R)
        xT_hi = sb("xT_hi", [P, 2, DC, P], F32R)
        xT_lo = sb("xT_lo", [P, 2, DC, P], F32R)
        st = sb("st", [P, 2, 6])
        mv = sb("mv", [P, 2])
        ve = sb("ve", [P, 2])
        rstd = sb("rstd", [P, 2])
        mv2 = sb("mv2", [P, 2, 2])
        rstd2 = sb("rstd2", [P, 2])
        nmax = sb("nmax", [P, H])
        rden = sb("rden", [P, H])
        held = sb("held", [P, 1])
        g_max = sb("g_max", [P, 1])
        g_sum = sb("g_sum", [P, 2])
        g_exp = sb("g_exp", [P, E])
        g_score = sb("g_score", [P, E + 8 - TOP])
        g_rest = sb("g_rest", [P, E + 8 - TOP])
        g_top = sb("g_top", [P, 8])
        g_sel = sb("g_sel", [P, E])
        comb = sb("comb", [P, 2, NE])

        scratch = sb("scratch", [P, SCRATCH])
        at = {"a": 0, "b": 0}

        def carve(stage, cols):
            first = at[stage]
            at[stage] += cols
            assert at[stage] <= SCRATCH
            return scratch[:, first:first + cols]

        probs = carve("a", 2 * 4 * P)
        probsT = carve("a", 2 * 4 * P)
        stage_up = carve("a", SL_UP)
        stage_dn = carve("a", SL_DN)
        x_in = carve("a", D)
        x_res = carve("a", D)
        xn = carve("a", D)
        xnT = carve("a", D)
        lat_n = carve("a", 2 * LAT)
        latT = carve("a", P)
        qT = carve("a", DC * P)
        vals = carve("a", H * (DH + 1)).rearrange("p (h c) -> p h c", h=H)
        att = carve("a", D)
        attT = carve("a", D)
        gw = attT[:, 0:DC * E]
        w_lat = carve("a", DC * 2 * LAT)
        w_latup = carve("a", 3 * D)
        w_out = carve("a", DC * D)

        kv = carve("b", B * PAIRS)
        hid = carve("b", HCOLS)
        mixed = carve("b", 512)
        sil = carve("b", 3 * I)
        xq = carve("b", D)
        xqT = carve("b", D)
        x2_in = carve("b", D)
        ctx_in = carve("b", D)
        toep_in = carve("b", 2 * P + 1)
        conv_o = carve("b", D)
        x3 = [carve("b", D) for _ in range(2)]
        x3n = carve("b", D)

        banks = [bank(f"bank{i}") for i in range(8)]
        score_b = banks[0:4]
        front_b, qv_b, pv_b, proj_b = banks[4:8]
        up_b = banks[0:3]
        turn_b = banks[3]
        down_b = banks[4]
        conv_b = banks[5:7]
        misc_b = banks[7]

        consts_loaded = sem("consts_loaded")
        consts_made = sem("consts_made")
        gw_split = sem("gw_split")
        x_loaded = sem("x_loaded")
        xres_loaded = sem("xres_loaded")
        stage_loaded = sem("stage_loaded")
        weights_split = sem("weights_split")
        x_stats = sem("x_stats")
        x_rstd = sem("x_rstd")
        x_normed = sem("x_normed")
        xn_turned = sem("xn_turned")
        xnT_ready = sem("xnT_ready")
        lat_done = sem("lat_done")
        lat_stats = sem("lat_stats")
        lat_rstd = sem("lat_rstd")
        lat_normed = sem("lat_normed")
        lat_turned = sem("lat_turned")
        latT_ready = sem("latT_ready")
        k_done = sem("k_done")
        v_done = sem("v_done")
        qv_done = sem("qv_done")
        q_taken = sem("q_taken")
        kT_zeroed = sem("kT_zeroed")
        k_taken = sem("k_taken")
        v_taken = sem("v_taken")
        scores_done = sem("scores_done")
        row_max = sem("row_max")
        exp_done = sem("exp_done")
        p_turned = sem("p_turned")
        pT_taken_v = sem("pT_taken_v")
        pT_taken_s = sem("pT_taken_s")
        weighed = sem("weighed")
        att_normed = sem("att_normed")
        att_turned = sem("att_turned")
        attT_ready = sem("attT_ready")
        proj_done = sem("proj_done")
        x2_made = sem("x2_made")
        x2_stored = sem("x2_stored")
        attn_vec = sem("attn_vec")
        attn_pool = sem("attn_pool")

        x2_loaded = sem("x2_loaded")
        ctx_loaded = sem("ctx_loaded")
        toep_loaded = sem("toep_loaded")
        q_stats = sem("q_stats")
        q_rstd = sem("q_rstd")
        q_normed = sem("q_normed")
        q_turned = sem("q_turned")
        qT_ready = sem("qT_ready")
        kv_made = sem("kv_made")
        kv_hi_ready = sem("kv_hi_ready")
        kv_lo_ready = sem("kv_lo_ready")
        toep_made = sem("toep_made")
        toep_hi_ready = sem("toep_hi_ready")
        toep_lo_ready = sem("toep_lo_ready")
        conv_done = sem("conv_done")
        conv_taken = sem("conv_taken")
        conv_mixed = sem("conv_mixed")
        conv_turned = sem("conv_turned")
        x3_made = sem("x3_made")
        x3_stats = sem("x3_stats")
        x3_rstd = sem("x3_rstd")
        x3_normed = sem("x3_normed")
        x3_turned = sem("x3_turned")
        xT_hi_ready = sem("xT_hi_ready")
        xT_lo_ready = sem("xT_lo_ready")
        gate_done = sem("gate_done")
        gate_max = sem("gate_max")
        gate_exp = sem("gate_exp")
        up_done = sem("up_done")
        silu_done = sem("silu_done")
        h_made = sem("h_made")
        h_turned = sem("h_turned")
        hT_hi_ready = sem("hT_hi_ready")
        hT_lo_ready = sem("hT_lo_ready")
        down_read = sem("down_read")
        out_made = sem("out_made")
        out_stored = sem("out_stored")
        front_vec = sem("front_vec")
        front_pool = sem("front_pool")

        ATTN_CONSTS = 6
        FRONT_LINKS = 13

        def hold(value):
            if not isinstance(value, int):
                nc.vector.memset(held[:, :], 0.0)

        block = ctx.enter_context(nc.Block())

        def all_tiles(eng, tile):
            tile(fixed(0), None, fixed(1), fixed(2))
            with eng.Fori(0, (HS - 4) // 2) as k:
                for o in (1, 2):
                    tile(looped(k, o), looped(k, o - 1), looped(k, o + 1), looped(k, o + 2))
            tile(fixed(HS - 3), fixed(HS - 4), fixed(HS - 2), fixed(HS - 1))
            tile(fixed(HS - 2), fixed(HS - 3), fixed(HS - 1), None)
            tile(fixed(HS - 1), fixed(HS - 2), None, None)

        @block.sync
        def _(sp):
            def load_x(b):
                wait(sp, x_normed, b)
                sp.dma_start(x_in, x[b]).then_inc(x_loaded, 16)

            def load_stage(b):
                wait(sp, weights_split, b * 4)
                sp.dma_start(stage_up, w_up[:, bass.ds(b * SL_UP, SL_UP)]).then_inc(stage_loaded, 16)
                sp.dma_start(stage_dn, w_dn[:, bass.ds(b * SL_DN, SL_DN)]).then_inc(stage_loaded, 16)

            def load_res(b):
                wait(sp, x2_stored, b * 16)
                sp.dma_start(x_res, x[b]).then_inc(xres_loaded, 16)

            def store_x2(b):
                sp.wait_ge(x2_made, b + 1)
                sp.dma_start(x2_dram[bass.ds(b * S, S), :], x_res).then_inc(x2_stored, 16)

            load_x(0)
            sp.dma_start(w_lat, lat_down).then_inc(consts_loaded, 16)
            sp.dma_start(gb[:, :], lat_gb).then_inc(consts_loaded, 16)
            sp.dma_start(w_latup, lat_up).then_inc(consts_loaded, 16)
            sp.dma_start(w_out, w_o).then_inc(consts_loaded, 16)
            sp.dma_start(gw, gate_w).then_inc(consts_loaded, 16)
            load_stage(0)
            load_x(1)
            def batch(b):
                load_res(b)
                load_x(b + 2)
                store_x2(b)
                load_stage(b + 1)

            batch(0)
            with sp.Fori(1, B - 2) as b:
                batch(b)
            load_res(B - 2)
            store_x2(B - 2)
            load_stage(B - 1)
            load_res(B - 1)
            store_x2(B - 1)

            sp.wait_ge(x2_stored, 16 * B)
            sp.wait_ge(weights_split, 4 * B)

            def load_x2(t):
                wait(sp, x3_made, t.n)
                sp.dma_start(x2_in, x2_heads[t.n]).then_inc(x2_loaded, 16)

            def load_toep(t):
                wait(sp, toep_lo_ready, t.n)
                sp.dma_start(toep_in, toep[t.n]).then_inc(toep_loaded, 16)

            def load_ctx(t):
                wait(sp, kv_made, t.n * 2)
                sp.dma_start(ctx_in, ctx_t[t.n]).then_inc(ctx_loaded, 16)

            def store_out(t):
                sp.wait_ge(out_made, t.n + 1)
                sp.dma_start(out_heads[t.n], x3[t.p]).then_inc(out_stored, 16)

            def tile(t, prev, nxt, after):
                if after:
                    load_toep(after)
                if prev:
                    store_out(prev)
                if after:
                    load_x2(after)
                    if not (isinstance(after.n, int) and after.n == HS - 1):
                        load_ctx(later(after))

            load_x2(fixed(0))
            load_toep(fixed(0))
            load_ctx(fixed(0))
            load_toep(fixed(1))
            load_ctx(fixed(1))
            load_x2(fixed(1))
            load_ctx(fixed(2))
            all_tiles(sp, tile)
            store_out(fixed(HS - 1))
            sp.wait_ge(out_stored, 16 * HS)

        @block.gpsimd
        def _(pool):
            g = nc.gpsimd
            g.memset(half_neg[:, :], -0.5).then_inc(attn_pool, 1)
            g.memset(eps[:, :], EPS).then_inc(attn_pool, 1)
            g.memset(ident[:, :], 0.0).then_inc(attn_pool, 1)
            g.memset(ident_b[:, :], 0.0).then_inc(attn_pool, 1)
            g.memset(causal[:, :], 0.0).then_inc(attn_pool, 1)
            g.memset(comb[:, :, E:NE], 1.0).then_inc(attn_pool, 1)
            g.memset(g_score[:, E:], -1.0).then_inc(attn_pool, 1)
            g.memset(vals[:, :, DH:DH + 1], 1.0).then_inc(attn_pool, 1)
            g.memset(kT, 0.0).then_inc(kT_zeroed, 1)
            pool.wait_ge(attn_pool, 8)
            g.affine_select(out=ident[:, :], in_=ident[:, :], compare_op=ALU.not_equal, fill=1.0, base=0,
                            pattern=[[-1, P]], channel_multiplier=1).then_inc(consts_made, 1)
            g.affine_select(out=ident_b[:, :], in_=ident_b[:, :], compare_op=ALU.not_equal, fill=1.0, base=0,
                            pattern=[[-1, P]], channel_multiplier=1).then_inc(consts_made, 1)
            g.affine_select(out=causal[:, :].rearrange("p (h k) -> p h k", h=4),
                            in_=causal[:, :].rearrange("p (h k) -> p h k", h=4), compare_op=ALU.is_ge,
                            fill=MASKED, base=0, pattern=[[0, 4], [-1, P]],
                            channel_multiplier=1).then_inc(consts_made, 1)
            pool.wait_ge(consts_loaded, 16 * 5)
            g.tensor_copy(gw_hi[:, :], gw).then_inc(gw_split, 1)
            pool.wait_ge(gw_split, 1)
            g.tensor_tensor(gw_lo[:, :], gw, gw_hi[:, :].bitcast(F32), ALU.subtract).then_inc(gw_split, 1)

            def rstd_x(b):
                pool.wait_ge(x_stats, b + 1)
                g.tensor_tensor(ve[:, 0:1], mv[:, 1:2], eps[:, 0:1], ALU.add).then_inc(attn_pool, 1)
                pool.wait_ge(attn_pool, b * 2 + 9)
                g.tensor_tensor(rstd[:, 0:1], ve[:, 0:1], half_neg[:, 0:1], ALU.pow).then_inc(x_rstd, 1)

            def rstd_lat(b):
                pool.wait_ge(x_rstd, b + 1)
                pool.wait_ge(lat_stats, b + 1)
                g.tensor_tensor(ve[:, :], mv2[:, :, 1], eps[:, :], ALU.add).then_inc(attn_pool, 1)
                pool.wait_ge(attn_pool, b * 2 + 10)
                g.tensor_tensor(rstd2[:, :], ve[:, :], half_neg[:, :], ALU.pow).then_inc(lat_rstd, 1)

            def split_up(b):
                pool.wait_ge(stage_loaded, b * 32 + 32)
                up = bass.ds(b * SL_UP, SL_UP)
                g.tensor_copy(wu_hi[:, up], stage_up).then_inc(weights_split, 1)
                pool.wait_ge(weights_split, b * 4 + 1)
                g.tensor_tensor(wu_lo[:, up], stage_up, wu_hi[:, up].bitcast(F32),
                                ALU.subtract).then_inc(weights_split, 1)

            def split_dn(b):
                dn = bass.ds(b * SL_DN, SL_DN)
                g.tensor_copy(wd_hi[:, dn], stage_dn).then_inc(weights_split, 1)
                pool.wait_ge(weights_split, b * 4 + 3)
                g.tensor_tensor(wd_lo[:, dn], stage_dn, wd_hi[:, dn].bitcast(F32),
                                ALU.subtract).then_inc(weights_split, 1)

            rstd_x(0)
            rstd_lat(0)
            rstd_x(1)
            with pool.Fori(0, B - 2) as b:
                rstd_lat(b + 1)
                split_up(b)
                rstd_x(b + 2)
                split_dn(b)
            rstd_lat(B - 1)
            for b in (B - 2, B - 1):
                split_up(b)
                split_dn(b)

            def rstd_of(t, stats, done):
                pool.wait_ge(stats, t.n + 1)
                g.tensor_tensor(ve[:, 0:1], mv[:, 1:2], eps[:, 0:1], ALU.add).then_inc(front_pool, 1)
                pool.wait_ge(front_pool, t.n * 2 + (1 if done is q_rstd else 2))
                g.tensor_tensor(rstd[:, 0:1], ve[:, 0:1], half_neg[:, 0:1], ALU.pow).then_inc(done, 1)

            def make_kv(t, lc):
                if lc == 0:
                    pool.wait_ge(ctx_loaded, t.n * 16 + 16)
                c = ctx_in[:, lc * P:(lc + 1) * P].rearrange("p (b i) -> p b i", b=B)
                shape = [P, B, HD, HD]
                wait(pool, kv_lo_ready, t.n * 2 + lc)
                g.tensor_tensor(kv.rearrange("p (b j i) -> p b j i", b=B, j=HD), c.unsqueeze(3).broadcast_to(shape),
                                c.unsqueeze(2).broadcast_to(shape), ALU.mult).then_inc(kv_made, 1)

            def kv_rest(t, lc):
                pool.wait_ge(kv_hi_ready, t.n * 2 + lc + 1)
                g.tensor_tensor(kv_lo[:, lc, :], kv, kv_hi[:, lc, :].bitcast(F32),
                                ALU.subtract).then_inc(kv_lo_ready, 1)

            def tile(t, prev, nxt, after):
                if after:
                    make_kv(after, 0)
                    kv_rest(after, 0)
                if nxt:
                    rstd_of(nxt, x3_stats, x3_rstd)
                if after:
                    make_kv(after, 1)
                    kv_rest(after, 1)
                    rstd_of(after, q_stats, q_rstd)

            rstd_of(fixed(0), q_stats, q_rstd)
            for lc in range(DC):
                make_kv(fixed(0), lc)
                kv_rest(fixed(0), lc)
            make_kv(fixed(1), 0)
            kv_rest(fixed(1), 0)
            rstd_of(fixed(0), x3_stats, x3_rstd)
            rstd_of(fixed(1), q_stats, q_rstd)
            make_kv(fixed(1), 1)
            kv_rest(fixed(1), 1)
            all_tiles(pool, tile)

        @block.scalar
        def _(act):
            a = nc.scalar

            def take_xnT(b):
                act.wait_ge(xn_turned, b + 1)
                wait(act, lat_done, b)
                a.copy(xnT, front_b[:, 0:D]).then_inc(xnT_ready, 1)

            def take_latT(b):
                act.wait_ge(lat_turned, b + 1)
                a.activation(latT, front_b[:, 3 * P:4 * P], ACT.Identity, bias=gb[:, 1:2],
                             scale=gb[:, 0:1]).then_inc(latT_ready, 1)

            def take_k(b):
                act.wait_ge(k_done, b + 1)
                wait(act, scores_done, b * 2)
                for r in range(4):
                    rows = slice(32 * r, 32 * r + 32)
                    a.copy(kT[rows, 4 * P * r:4 * P * (r + 1)], front_b[rows, :]).then_inc(k_taken, 1)

            def exps(b, r):
                act.wait_ge(row_max, b * 4 + r + 1)
                wait(act, p_turned, b * 4 + r - 1)
                for s in range(4 * r, 4 * r + 4):
                    ins = a.activation(probs[:, (s % 8) * P:(s % 8 + 1) * P], score_b[r][:, (s % 4) * P:(s % 4 + 1) * P],
                                       ACT.Exp, bias=nmax[:, s:s + 1])
                ins.then_inc(exp_done, 1)

            def batch(b, n1, n2):
                exps(b, 2)
                if n1 is not None:
                    take_latT(n1)
                exps(b, 3)
                act.wait_ge(p_turned, b * 4 + 4)
                act.wait_ge(weighed, b * 4 + 2)
                a.copy(probsT[:, 4 * P:8 * P], score_b[3][:, :]).then_inc(pT_taken_s, 1)
                if n1 is not None:
                    take_k(n1)
                act.wait_ge(att_turned, b + 1)
                if isinstance(b, int) and b == 0:
                    act.wait_ge(gw_split, 2)
                a.copy(attT, proj_b[:, 0:D]).then_inc(attT_ready, 1)
                if n1 is not None:
                    exps(n1, 0)
                if n2 is not None:
                    take_xnT(n2)
                if n1 is not None:
                    exps(n1, 1)

            act.wait_ge(consts_loaded, 16 * 5)
            take_xnT(0)
            take_latT(0)
            act.wait_ge(kT_zeroed, 1)
            take_k(0)
            take_xnT(1)
            exps(0, 0)
            exps(0, 1)
            batch(0, 1, 2)
            with act.Fori(1, B - 2) as b:
                batch(b, b + 1, b + 2)
            batch(B - 2, B - 1, None)
            batch(B - 1, None, None)

            def kv_round(t, lc):
                act.wait_ge(kv_made, t.n * 2 + lc + 1)
                wait(act, conv_done, t.n * 4)
                a.copy(kv_hi[:, lc, :], kv).then_inc(kv_hi_ready, 1)

            def take_qT(t):
                act.wait_ge(q_turned, t.n + 1)
                wait(act, conv_mixed, t.n * 4)
                a.copy(xqT, misc_b[:, 0:D]).then_inc(qT_ready, 1)

            def toep_round(t):
                act.wait_ge(toep_made, t.n + 1)
                wait(act, conv_done, t.n * 4)
                a.copy(t_hi[:, :], toep_in[:, 0:2 * P]).then_inc(toep_hi_ready, 1)

            def x3T_round(t):
                act.wait_ge(x3_turned, t.n + 1)
                a.copy(xT_hi[:, t.p, :, :], misc_b[:, 0:D].rearrange("p (c n) -> p c n", c=DC)).then_inc(xT_hi_ready, 1)

            def gate_exponent(t):
                act.wait_ge(gate_max, t.n + 1)
                a.activation(g_exp[:, :], misc_b[:, D:D + E], ACT.Exp, bias=g_max[:, 0:1]).then_inc(gate_exp, 1)

            def silu(t, e):
                act.wait_ge(up_done, t.n * NE + e + 1)
                a.activation(sil[:, (e % 3) * I:(e % 3 + 1) * I], up_b[e % 3][:, 0:I], ACT.Silu).then_inc(silu_done, 1)

            def h_round(t, grp):
                act.wait_ge(h_turned, t.n * NG + grp + 1)
                wait(act, down_read, t.n * NG + grp)
                n = min(4, NCH - 4 * grp)
                rows = P if grp < NG - 1 else LAST
                a.copy(hT_hi[0:rows, 0:n, :],
                       turn_b[0:rows, 0:n * P].rearrange("p (c n) -> p c n", c=n)).then_inc(hT_hi_ready, 1)

            def tile(t, prev, nxt, after):
                for e in range(NE):
                    silu(t, e)
                    for grp, s in TAIL_TURN_AT.items():
                        if prev and s == e:
                            h_round(prev, grp)
                    for grp, s in TURN_AT.items():
                        if s == e:
                            h_round(t, grp)
                    if nxt and e == 0:
                        take_qT(nxt)
                    if after and e == 7:
                        kv_round(after, 0)
                    if after and e == 10:
                        toep_round(after)
                    if nxt and e == 12:
                        x3T_round(nxt)
                    if nxt and e == 14:
                        gate_exponent(nxt)
                    if after and e == 15:
                        kv_round(after, 1)

            take_qT(fixed(0))
            toep_round(fixed(0))
            kv_round(fixed(0), 0)
            kv_round(fixed(0), 1)
            kv_round(fixed(1), 0)
            toep_round(fixed(1))
            x3T_round(fixed(0))
            gate_exponent(fixed(0))
            kv_round(fixed(1), 1)
            all_tiles(act, tile)
            h_round(fixed(HS - 1), 5)
            h_round(fixed(HS - 1), 6)

        @block.vector
        def _(dve):
            v = nc.vector

            def norm_x(b):
                dve.wait_ge(x_loaded, b * 16 + 16)
                v.bn_stats(st[:, 0, :], x_in).then_inc(attn_vec, 1)
                dve.wait_ge(attn_vec, 1 if isinstance(b, int) and b == 0 else b * 3)
                hold(b)
                v.bn_aggr(mv[:, :], st[:, 0, :]).then_inc(x_stats, 1)
                dve.wait_ge(x_rstd, b + 1)
                wait(dve, xn_turned, b)
                v.tensor_scalar(xn, x_in, mv[:, 0:1], rstd[:, 0:1], ALU.subtract, ALU.mult).then_inc(x_normed, 1)

            def lat_statistics(b):
                dve.wait_ge(lat_done, b + 1)
                for i in range(2):
                    ins = v.bn_stats(st[:, i, :], front_b[:, 2 * P + i * LAT:2 * P + (i + 1) * LAT])
                ins.then_inc(attn_vec, 1)
                dve.wait_ge(attn_vec, 2 if isinstance(b, int) and b == 0 else b * 3 + 1)
                hold(b)
                for i in range(2):
                    ins = v.bn_aggr(mv2[:, i, :], st[:, i, :])
                ins.then_inc(lat_stats, 1)

            def norm_lat(b):
                dve.wait_ge(lat_rstd, b + 1)
                wait(dve, lat_turned, b)
                for i in range(2):
                    ins = v.tensor_scalar(lat_n[:, i * LAT:(i + 1) * LAT],
                                          front_b[:, 2 * P + i * LAT:2 * P + (i + 1) * LAT],
                                          mv2[:, i, 0:1], rstd2[:, i:i + 1], ALU.subtract, ALU.mult)
                ins.then_inc(lat_normed, 1)

            def take_q(b):
                dve.wait_ge(qv_done, b + 1)
                wait(dve, scores_done, b * 2)
                v.tensor_scalar(qT, qv_b[:, 0:D], float(DH) ** -0.5, None, ALU.mult).then_inc(q_taken, 1)

            def take_v(b):
                wait(dve, weighed, b * 4)
                v.tensor_copy(vals[:, :, 0:DH],
                              qv_b[:, D:2 * D].rearrange("p (h c) -> p h c", h=H)).then_inc(v_taken, 1)

            def take_pT(b, r):
                dve.wait_ge(p_turned, b * 4 + r + 1)
                wait(dve, weighed, b * 4 + r - 1)
                v.tensor_copy(probsT[:, (r % 2) * 4 * P:(r % 2 + 1) * 4 * P], score_b[r][:, :]).then_inc(pT_taken_v, 1)

            def row_maxima(b):
                for r in range(4):
                    dve.wait_ge(scores_done, b * 2 + r // 2 + 1)
                    wait(dve, exp_done, b * 4 + r - 3)
                    v.tensor_reduce(nmax[:, 4 * r:4 * r + 4], score_b[r][:, :].rearrange("p (h k) -> p h k", h=4),
                                    AX_X, ALU.max, negate=True).then_inc(row_max, 1)

            def batch(b, n1, n2):
                if n1 is not None:
                    lat_statistics(n1)
                take_pT(b, 0)
                if n1 is not None:
                    norm_lat(n1)
                take_pT(b, 1)
                take_pT(b, 2)
                if n1 is not None:
                    take_q(n1)
                dve.wait_ge(weighed, b * 4 + 4)
                o = pv_b[:, 0:H * (DH + 1)].rearrange("p (h c) -> p h c", h=H)
                v.reciprocal(rden[:, :], o[:, :, DH]).then_inc(attn_vec, 1)
                if n1 is not None:
                    take_v(n1)
                dve.wait_ge(attn_vec, b * 3 + 5 if n1 is not None else b * 3 + 3)
                wait(dve, att_turned, b)
                v.tensor_tensor(att.rearrange("p (h c) -> p h c", h=H), o[:, :, 0:DH],
                                rden[:, :].unsqueeze(2).broadcast_to([P, H, DH]), ALU.mult).then_inc(att_normed, 1)
                if n2 is not None:
                    norm_x(n2)
                if n1 is not None:
                    row_maxima(n1)
                dve.wait_ge(proj_done, b + 1)
                dve.wait_ge(xres_loaded, b * 16 + 16)
                v.tensor_tensor(x_res, proj_b[:, D:2 * D], x_res, ALU.add).then_inc(x2_made, 1)

            norm_x(0)
            lat_statistics(0)
            norm_lat(0)
            norm_x(1)
            take_q(0)
            take_v(0)
            row_maxima(0)
            batch(0, 1, 2)
            with dve.Fori(1, B - 2) as b:
                batch(b, b + 1, b + 2)
            batch(B - 2, B - 1, None)
            batch(B - 1, None, None)

            def statistics(src, done, chain):
                chain.link(v.bn_stats(st[:, 0, :], src))
                hold(chain.base)
                v.bn_aggr(mv[:, :], st[:, 0, :]).then_inc(done, 1)

            def norm_q(t, chain):
                dve.wait_ge(x2_loaded, t.n * 16 + 16)
                statistics(x2_in, q_stats, chain)
                dve.wait_ge(q_rstd, t.n + 1)
                v.tensor_scalar(xq, x2_in, mv[:, 0:1], rstd[:, 0:1], ALU.subtract, ALU.mult).then_inc(q_normed, 1)

            def toep_diag(t):
                w = toep_in
                dve.wait_ge(toep_loaded, t.n * 16 + 16)
                v.scalar_tensor_tensor(out=w[:, 0:P], in0=ident[:, :], scalar=w[:, 2 * P:2 * P + 1], in1=w[:, 0:P],
                                       op0=ALU.mult, op1=ALU.add).then_inc(toep_made, 1)

            def toep_rest(t):
                dve.wait_ge(toep_hi_ready, t.n + 1)
                v.tensor_tensor(t_lo[:, :], toep_in[:, 0:2 * P], t_hi[:, :].bitcast(F32),
                                ALU.subtract).then_inc(toep_lo_ready, 1)

            def mix(t, u):
                lc, n = divmod(u, 2)
                if u == 0:
                    dve.wait_ge(qT_ready, t.n + 1)
                dve.wait_ge(conv_done, t.n * 4 + u + 1)
                wait(dve, conv_mixed, t.n * 4 + u)
                shape = [P, B // 2, HD, HD]
                m = mixed.rearrange("p (b j i) -> p b j i", b=B // 2, j=HD)
                q = xqT[:, lc * P + n * 64:lc * P + (n + 1) * 64].rearrange("p (b i) -> p b i", b=B // 2)
                v.tensor_tensor(m, conv_b[u % 2][:, :].rearrange("p (b j i) -> p b j i", b=B // 2, j=HD),
                                q.unsqueeze(2).broadcast_to(shape), ALU.mult).then_inc(conv_taken, 1)
                dve.wait_ge(conv_taken, t.n * 4 + u + 1)
                v.tensor_reduce(conv_o[:, lc * P + n * 64:lc * P + (n + 1) * 64],
                                mixed.rearrange("p (o i) -> p o i", i=HD),
                                AX_X, ALU.add).then_inc(conv_mixed, 1)

            def make_x3(t, chain):
                dve.wait_ge(conv_turned, t.n + 1)
                wait(dve, out_stored, t.n * 16 - 16)
                v.tensor_tensor(x3[t.p], misc_b[:, 0:D], x2_in, ALU.add).then_inc(x3_made, 1)
                dve.wait_ge(x3_made, t.n + 1)
                statistics(x3[t.p], x3_stats, chain)

            def norm_x3(t):
                dve.wait_ge(x3_rstd, t.n + 1)
                v.tensor_scalar(x3n, x3[t.p], mv[:, 0:1], rstd[:, 0:1], ALU.subtract, ALU.mult).then_inc(x3_normed, 1)

            def x3T_rest(t):
                dve.wait_ge(xT_hi_ready, t.n + 1)
                v.tensor_tensor(xT_lo[:, t.p, :, :], misc_b[:, 0:D].rearrange("p (c n) -> p c n", c=DC),
                                xT_hi[:, t.p, :, :].bitcast(F32), ALU.subtract).then_inc(xT_lo_ready, 1)

            def gating(t, chain):
                dve.wait_ge(gate_done, t.n + 1)
                v.tensor_reduce(g_max[:, :], misc_b[:, D:D + E], AX_X, ALU.max, negate=True).then_inc(gate_max, 1)
                dve.wait_ge(gate_exp, t.n + 1)
                chain.link(v.reduce_sum(g_sum[:, 0:1], g_exp[:, :], AX_X))
                chain.link(v.reciprocal(g_sum[:, 1:2], g_sum[:, 0:1]))
                chain.link(v.tensor_scalar(g_score[:, 0:E], g_exp[:, :], g_sum[:, 1:2], None, ALU.mult))
                hold(chain.base)
                chain.link(v.max(g_top[:, :], g_score[:, 0:E]))
                chain.link(v.memset(g_top[:, TOP:8], -1.0))
                hold(chain.base)
                chain.link(v.match_replace(g_rest[:, :], g_top[:, :], g_score[:, :], 0.0))
                chain.link(v.tensor_tensor(g_sel[:, :], g_score[:, 0:E], g_rest[:, 0:E], ALU.subtract))
                chain.link(v.reduce_sum(g_sum[:, 0:1], g_sel[:, :], AX_X))
                chain.link(v.tensor_scalar(g_sum[:, 0:1], g_sum[:, 0:1], 1e-20, None, ALU.add))
                chain.link(v.reciprocal(g_sum[:, 1:2], g_sum[:, 0:1]))
                chain.link(v.tensor_scalar(comb[:, t.p, 0:E], g_sel[:, :], g_sum[:, 1:2], None, ALU.mult))

            def hidden(t, e):
                dve.wait_ge(silu_done, t.n * NE + e + 1)
                grp = (I * (e + 1) - 1) // 512
                wait(dve, h_turned, t.n * NG - NG + grp + 1)
                v.scalar_tensor_tensor(out=hid[:, e * I:(e + 1) * I], in0=sil[:, (e % 3) * I:(e % 3 + 1) * I],
                                       scalar=comb[:, t.p, e:e + 1], in1=up_b[e % 3][:, I:2 * I],
                                       op0=ALU.mult, op1=ALU.mult).then_inc(h_made, 1)

            def h_rest(t, grp):
                dve.wait_ge(hT_hi_ready, t.n * NG + grp + 1)
                n = min(4, NCH - 4 * grp)
                rows = P if grp < NG - 1 else LAST
                v.tensor_tensor(hT_lo[0:rows, 0:n, :], turn_b[0:rows, 0:n * P].rearrange("p (c n) -> p c n", c=n),
                                hT_hi[0:rows, 0:n, :].bitcast(F32), ALU.subtract).then_inc(hT_lo_ready, 1)

            def finish(t):
                dve.wait_ge(down_read, t.n * NG + NG)
                v.tensor_tensor(x3[t.p], down_b[:, 0:D], x3[t.p], ALU.add).then_inc(out_made, 1)

            def tile(t, prev, nxt, after):
                chain = Chain(dve, front_vec, nxt.n * FRONT_LINKS + 1) if nxt else None
                for e in range(NE):
                    hidden(t, e)
                    for grp, s in TAIL_TURN_AT.items():
                        if prev and s == e:
                            h_rest(prev, grp)
                    for grp, s in TURN_AT.items():
                        if s == e:
                            h_rest(t, grp)
                    if prev and e == 6:
                        finish(prev)
                    for u, s in MIX_AT.items():
                        if nxt and s == e:
                            mix(nxt, u)
                    if nxt and e == 9:
                        make_x3(nxt, chain)
                    if nxt and e == 10:
                        norm_x3(nxt)
                    if after and e == 9:
                        toep_diag(after)
                    if after and e == 11:
                        toep_rest(after)
                    if nxt and e == 12:
                        x3T_rest(nxt)
                    if nxt and e == 14:
                        gating(nxt, chain)
                    if e == 16 and nxt:
                        if after:
                            norm_q(after, chain)
                        chain.close(FRONT_LINKS if after else FRONT_LINKS - 1)

            dve.wait_ge(consts_made, 3)
            t0, t1 = fixed(0), fixed(1)
            chain = Chain(dve, front_vec, 0)
            norm_q(t0, chain)
            chain.close(1)
            toep_diag(t0)
            toep_rest(t0)
            for u in range(4):
                mix(t0, u)
            toep_diag(t1)
            toep_rest(t1)
            chain = Chain(dve, front_vec, 1)
            make_x3(t0, chain)
            norm_x3(t0)
            x3T_rest(t0)
            gating(t0, chain)
            norm_q(t1, chain)
            chain.close(FRONT_LINKS)
            all_tiles(dve, tile)
            h_rest(fixed(HS - 1), 5)
            h_rest(fixed(HS - 1), 6)
            finish(fixed(HS - 1))

        @block.tensor
        def _(pe):
            mm = nc.tensor.matmul

            def turn_x(b):
                pe.wait_ge(x_normed, b + 1)
                wait(pe, k_taken, b * 4)
                for c in range(DC):
                    ins = nc.tensor.transpose(front_b[:, c * P:(c + 1) * P], xn[:, c * P:(c + 1) * P], ident[:, :])
                ins.then_inc(xn_turned, 1)

            def latents(b):
                pe.wait_ge(xnT_ready, b + 1)
                for c in range(DC):
                    ins = mm(front_b[:, 2 * P:3 * P], xnT[:, c * P:(c + 1) * P], w_lat[:, c * P:(c + 1) * P],
                             start=(c == 0), stop=(c == DC - 1))
                ins.then_inc(lat_done, 1)

            def turn_lat(b):
                pe.wait_ge(lat_normed, b + 1)
                nc.tensor.transpose(front_b[:, 3 * P:4 * P], lat_n, ident[:, :]).then_inc(lat_turned, 1)

            def keys(b):
                pe.wait_ge(latT_ready, b + 1)
                for c in range(DC):
                    for v in range(2):
                        o, w = (2 * c + v) * P, D + (v * DC + c) * P
                        ins = mm(front_b[:, o:o + P], w_latup[LAT:, w:w + P], latT[LAT:, :],
                                 start=True, stop=True)
                ins.then_inc(k_done, 1)

            def values(b):
                pe.wait_ge(latT_ready, b + 1)
                wait(pe, q_taken, b)
                wait(pe, v_taken, b)
                mm(qv_b[:, D:2 * D], latT[LAT:2 * LAT, :], w_latup[LAT:2 * LAT, 0:D],
                   start=True, stop=True).then_inc(v_done, 1)

            def queries(b):
                pe.wait_ge(v_done, b + 1)
                for c in range(DC):
                    ins = mm(qv_b[:, c * P:(c + 1) * P], w_latup[0:LAT, c * P:(c + 1) * P], latT[0:LAT, :],
                             start=True, stop=True)
                ins.then_inc(qv_done, 1)

            def scores(b, half):
                banks_now = (2 * half, 2 * half + 1)
                pe.wait_ge(q_taken, b + 1)
                pe.wait_ge(k_taken, b * 4 + 2 * half + 2)
                if half == 0:
                    wait(pe, pT_taken_v, b * 3 - 1)
                else:
                    wait(pe, pT_taken_v, b * 3)
                    wait(pe, pT_taken_s, b)
                for r in banks_now:
                    mm(score_b[r][:, :], ident_b[:, :], causal[:, :], start=True, stop=False, skip_group_check=True)
                for c in range(DC):
                    for r in banks_now:
                        o = 2 * c * P
                        ins = mm(score_b[r][:, o:o + 2 * P], qT[:, c * P:(c + 1) * P],
                                 kT[:, 4 * P * r + o:4 * P * r + o + 2 * P],
                                 start=False, stop=(c == 1), skip_group_check=True)
                ins.then_inc(scores_done, 1)

            def turn_p(b, r):
                pe.wait_ge(exp_done, b * 4 + r + 1)
                for s in range(4):
                    ins = nc.tensor.transpose(score_b[r][:, s * P:(s + 1) * P],
                                              probs[:, (4 * (r % 2) + s) * P:(4 * (r % 2) + s + 1) * P], ident[:, :])
                ins.then_inc(p_turned, 1)

            def weigh(b, r):
                if r == 0:
                    pe.wait_ge(v_taken, b + 1)
                    wait(pe, att_normed, b)
                if r < 3:
                    pe.wait_ge(pT_taken_v, b * 3 + r + 1)
                else:
                    pe.wait_ge(pT_taken_s, b + 1)
                for s in range(4):
                    h = 8 * (s // 2) + 2 * r + s % 2
                    o = h * (DH + 1)
                    q = (4 * (r % 2) + s) * P
                    ins = mm(pv_b[:, o:o + DH + 1], probsT[:, q:q + P], vals[:, h, :], start=True, stop=True)
                ins.then_inc(weighed, 1)

            def project_turn(b):
                pe.wait_ge(att_normed, b + 1)
                wait(pe, x2_made, b)
                for c in range(DC):
                    ins = nc.tensor.transpose(proj_b[:, c * P:(c + 1) * P], att[:, c * P:(c + 1) * P], ident[:, :])
                ins.then_inc(att_turned, 1)

            def project(b):
                pe.wait_ge(attT_ready, b + 1)
                for c in range(DC):
                    ins = mm(proj_b[:, D:2 * D], attT[:, c * P:(c + 1) * P], w_out[:, c * D:(c + 1) * D],
                             start=(c == 0), stop=(c == DC - 1))
                ins.then_inc(proj_done, 1)

            def batch(b, n1, n2):
                if n1 is not None:
                    latents(n1)
                turn_p(b, 0)
                turn_p(b, 1)
                weigh(b, 0)
                if n1 is not None:
                    turn_lat(n1)
                turn_p(b, 2)
                weigh(b, 1)
                turn_p(b, 3)
                if n1 is not None:
                    keys(n1)
                weigh(b, 2)
                if n1 is not None:
                    values(n1)
                    queries(n1)
                weigh(b, 3)
                if n1 is not None:
                    scores(n1, 0)
                project_turn(b)
                if n1 is not None:
                    scores(n1, 1)
                if n2 is not None:
                    turn_x(n2)
                project(b)

            pe.wait_ge(consts_loaded, 16 * 5)
            pe.wait_ge(consts_made, 3)
            turn_x(0)
            latents(0)
            turn_lat(0)
            keys(0)
            values(0)
            queries(0)
            turn_x(1)
            scores(0, 0)
            scores(0, 1)
            batch(0, 1, 2)
            with pe.Fori(1, B - 2) as b:
                batch(b, b + 1, b + 2)
            batch(B - 2, B - 1, None)
            batch(B - 1, None, None)

            def three(out_ap, stat, mov, first, last):
                (s_hi, s_lo), (m_hi, m_lo) = stat, mov
                mm(out_ap, s_hi, m_hi, start=first, stop=False)
                mm(out_ap, s_hi, m_lo, start=False, stop=False)
                return mm(out_ap, s_lo, m_hi, start=False, stop=last)

            def turn_q(t):
                pe.wait_ge(q_normed, t.n + 1)
                wait(pe, gate_exp, t.n)
                for c in range(DC):
                    ins = nc.tensor.transpose(misc_b[:, c * P:(c + 1) * P], xq[:, c * P:(c + 1) * P], ident[:, :])
                ins.then_inc(q_turned, 1)

            def conv(t, u):
                lc, n = divmod(u, 2)
                if u == 0:
                    pe.wait_ge(toep_lo_ready, t.n + 1)
                    pe.wait_ge(kv_lo_ready, t.n * 2 + 2)
                wait(pe, conv_taken, t.n * 4 + u - 1)
                cols = slice(n * 512, (n + 1) * 512)
                for mc in range(lc + 1):
                    tap = slice((lc - mc) * P, (lc - mc + 1) * P)
                    ins = three(conv_b[u % 2][:, :], (t_hi[:, tap], t_lo[:, tap]),
                                (kv_hi[:, mc, cols], kv_lo[:, mc, cols]), mc == 0, mc == lc)
                ins.then_inc(conv_done, 1)

            def turn_conv(t):
                pe.wait_ge(conv_mixed, t.n * 4 + 4)
                pe.wait_ge(qT_ready, t.n + 1)
                for c in range(DC):
                    ins = nc.tensor.transpose(misc_b[:, c * P:(c + 1) * P], conv_o[:, c * P:(c + 1) * P], ident[:, :])
                ins.then_inc(conv_turned, 1)

            def turn_x3(t):
                pe.wait_ge(x3_normed, t.n + 1)
                for c in range(DC):
                    ins = nc.tensor.transpose(misc_b[:, c * P:(c + 1) * P], x3n[:, c * P:(c + 1) * P], ident[:, :])
                ins.then_inc(x3_turned, 1)

            def gate(t):
                pe.wait_ge(xT_lo_ready, t.n + 1)
                for c in range(DC):
                    ins = three(misc_b[:, D:D + E], (xT_hi[:, t.p, c, :], xT_lo[:, t.p, c, :]),
                                (gw_hi[:, c * E:(c + 1) * E], gw_lo[:, c * E:(c + 1) * E]), c == 0, c == DC - 1)
                ins.then_inc(gate_done, 1)

            def up(t, e):
                if e == 0:
                    pe.wait_ge(xT_lo_ready, t.n + 1)
                wait(pe, h_made, t.n * NE + e - 2)
                for c in range(DC):
                    o = (c * NE + e) * UC
                    ins = three(up_b[e % 3][:, 0:UC], (xT_hi[:, t.p, c, :], xT_lo[:, t.p, c, :]),
                                (wu_hi[:, o:o + UC], wu_lo[:, o:o + UC]), c == 0, c == DC - 1)
                ins.then_inc(up_done, 1)

            def turn_h(t, grp):
                last_expert = (min(512 * (grp + 1), HCOLS) - 1) // I
                pe.wait_ge(h_made, t.n * NE + last_expert + 1)
                wait(pe, hT_lo_ready, t.n * NG + grp)
                for j in range(4 * grp, min(4 * grp + 4, NCH)):
                    rows = P if j < NCH - 1 else LAST
                    ins = nc.tensor.transpose(turn_b[0:rows, (j % 4) * P:(j % 4 + 1) * P], hid[:, j * P:j * P + rows],
                                              ident[:, :])
                ins.then_inc(h_turned, 1)

            def down(t, grp):
                pe.wait_ge(hT_lo_ready, t.n * NG + grp + 1)
                if grp == 0:
                    wait(pe, out_made, t.n)
                for j in range(4 * grp, min(4 * grp + 4, NCH)):
                    rows = P if j < NCH - 1 else LAST
                    ins = three(down_b[:, 0:D], (hT_hi[0:rows, j % 4, :], hT_lo[0:rows, j % 4, :]),
                                (wd_hi[0:rows, j * D:(j + 1) * D], wd_lo[0:rows, j * D:(j + 1) * D]),
                                j == 0, j == NCH - 1)
                ins.then_inc(down_read, 1)

            def tile(t, prev, nxt, after):
                for e in range(NE):
                    up(t, e)
                    for grp, s in TAIL_DOWN_AT.items():
                        if prev and s == e:
                            down(prev, grp)
                    for grp, s in DOWN_AT.items():
                        if s == e:
                            down(t, grp)
                    if nxt and e == 0:
                        turn_q(nxt)
                    for grp, s in TAIL_TURN_AT.items():
                        if prev and s == e:
                            turn_h(prev, grp)
                    for grp, s in TURN_AT.items():
                        if s == e:
                            turn_h(t, grp)
                    for u, s in CONV_AT.items():
                        if nxt and s == e:
                            conv(nxt, u)
                    if nxt and e == 9:
                        turn_conv(nxt)
                    if nxt and e == 12:
                        turn_x3(nxt)
                    if nxt and e == 13:
                        gate(nxt)

            pe.wait_ge(gw_split, 2)
            t0 = fixed(0)
            turn_q(t0)
            for u in range(4):
                conv(t0, u)
            turn_conv(t0)
            turn_x3(t0)
            gate(t0)
            pe.wait_ge(weights_split, 4 * B)
            all_tiles(pe, tile)
            end = fixed(HS - 1)
            down(end, 4)
            turn_h(end, 5)
            down(end, 5)
            turn_h(end, 6)
            down(end, 6)


def kernel(x, ctx_2048, L0_attn_W_dq, L0_attn_W_uq, L0_attn_q_ln_g, L0_attn_q_ln_b, L0_attn_W_dkv, L0_attn_W_ukv,
           L0_attn_kv_ln_g, L0_attn_kv_ln_b, L0_attn_W_o, L0_xattn_ssm_kernel, L0_xattn_D, L0_ffn_gate_w,
           L0_ffn_w13, L0_ffn_w2, L0_ffn_sw13, L0_ffn_sw2):
    import numpy as np
    import concourse.bacc as bacc
    from concourse.bass_utils import run_bass_kernel_spmd

    f = np.float32
    a = {k: np.asarray(w) for k, w in dict(
        x=x, ctx=ctx_2048, wdq=L0_attn_W_dq, wuq=L0_attn_W_uq, qg=L0_attn_q_ln_g, qb=L0_attn_q_ln_b,
        wdkv=L0_attn_W_dkv, wukv=L0_attn_W_ukv, kg=L0_attn_kv_ln_g, kb=L0_attn_kv_ln_b, wo=L0_attn_W_o,
        taps=L0_xattn_ssm_kernel, skip=L0_xattn_D, gate=L0_ffn_gate_w, w13=L0_ffn_w13, w2=L0_ffn_w2,
        sw13=L0_ffn_sw13, sw2=L0_ffn_sw2).items()}

    def chunked(w):
        return np.ascontiguousarray(w.reshape(-1, P, w.shape[1]).transpose(1, 0, 2).reshape(P, -1))

    w_k = np.zeros((LAT, 2, H, DH), f)
    for v in range(2):
        w_k[:, v, v::2] = a["wukv"][:, 0:D].reshape(LAT, H, DH)[:, v::2]
    lat_up = np.zeros((P, 3 * D), f)
    lat_up[0:LAT, 0:D] = a["wuq"]
    lat_up[LAT:, D:] = w_k.reshape(LAT, 2 * D)
    lat_up[LAT:, 0:D] = a["wukv"][:, D:]
    padded = np.concatenate([np.zeros((HS, P - 1), f), a["taps"]], axis=1)
    toep = np.empty((HS, P, 2 * P + 1), f)
    toep[:, :, 0:2 * P] = padded[:, P - 1 - np.arange(P)[:, None] + np.arange(2 * P)[None, :]]
    toep[:, :, 2 * P] = a["skip"][:, None]
    ctx_t = a["ctx"].reshape(B, HS, HD, DC, P).transpose(1, 4, 3, 0, 2).reshape(HS, P, DC * P)
    s13 = a["sw13"].reshape(2, NS, I, D).transpose(1, 0, 2, 3).reshape(NS, UC, D)
    w13 = np.concatenate([a["w13"], s13], axis=0)
    w_up = w13.reshape(NE, UC, DC, P).transpose(3, 2, 0, 1).reshape(P, NW_UP)
    w2 = np.concatenate([a["w2"].transpose(0, 2, 1).reshape(E * I, D), a["sw2"].T,
                         np.zeros((NCH * P - HCOLS, D), f)], axis=0)

    arrays = dict(
        x=a["x"], ctx_t=ctx_t, lat_down=chunked(np.concatenate([a["wdq"], a["wdkv"]], axis=1)),
        lat_gb=np.stack([np.concatenate([a["qg"], a["kg"]]), np.concatenate([a["qb"], a["kb"]])], axis=1),
        lat_up=lat_up, w_o=chunked(a["wo"].T), toep=toep, gate_w=chunked(a["gate"].T), w_up=w_up, w_dn=chunked(w2))
    nc = bacc.Bacc("TRN2", target_bir_lowering=False, num_devices=1)
    arrays = {f"in_{k}": np.ascontiguousarray(w) for k, w in arrays.items()}
    args = [nc.dram_tensor(k, w.shape, F32, kind="ExternalInput").ap() for k, w in arrays.items()]
    out = nc.dram_tensor("out_x", (B, S, D), F32, kind="ExternalOutput").ap()
    build(nc, *args, out)
    r = run_bass_kernel_spmd(nc, [arrays], core_ids=[0])
    return r.results[0]["out_x"]
```

```python
import math
from contextlib import ExitStack

import concourse.bass as bass
from concourse import mybir

F32 = mybir.dt.float32
F32R = mybir.dt.float32r
BF16 = mybir.dt.bfloat16
ALU = mybir.AluOpType
ACT = mybir.ActivationFunctionType
AX_X = mybir.AxisListType.X

P = 128
B, S, D = 16, 128, 256
DC = D // P
LAT = 64
H, DH = 16, 16
HS, HD = 16, 8
E, I = 16, 176
TOP = 6
NS = 2
NE = E + NS
UC = 2 * I
NW_UP = DC * NE * UC
HCOLS = NE * I
NCH = -(-HCOLS // P)
LAST = HCOLS - (NCH - 1) * P
NW_DN = NCH * D
SL_UP, SL_DN = NW_UP // B, NW_DN // B
NG = -(-NCH // 4)
EPS = 1e-5
MASKED = -1e30
SCRATCH = 7632
OFFS = HD // 2 + 1
MIRROR = HD // 2 - 1
PAIRS = OFFS * HD
HW = HD + HD // 2
ZW = HD + MIRROR
SLOTS = OFFS + MIRROR
HALF = B // 2 * PAIRS

TURN_AT = {0: 5, 1: 8, 2: 11, 3: 14, 4: 16}
DOWN_AT = {0: 7, 1: 10, 2: 13, 3: 16}
TAIL_TURN_AT = {5: 1, 6: 3}
TAIL_DOWN_AT = {4: 0, 5: 3, 6: 5}
CONV_AT = {0: 1, 1: 2, 2: 4, 3: 6}
MIX_AT = {0: 2, 1: 4, 2: 6, 3: 7}


class Tile:

    def __init__(self, n, p, half):
        self.n, self.p, self.half = n, p, half


def fixed(n):
    return Tile(n, n % 2, n // 2)


def looped(k, off):
    return Tile(k * 2 + off, off % 2, k + off // 2)


def later(t):
    return Tile(t.n + 1, 1 - t.p, t.half + t.p)


def wait(eng, sem, value):
    if not isinstance(value, int) or value > 0:
        eng.wait_ge(sem, value)


class Chain:

    def __init__(self, eng, sem, base):
        self.eng, self.sem, self.base, self.k = eng, sem, base, 0

    def link(self, ins):
        ins.then_inc(self.sem, 1)
        self.k += 1
        self.eng.wait_ge(self.sem, self.base + self.k)

    def close(self, links):
        assert self.k == links, (self.k, links)


def windows(cols, n):
    return bass.AP(cols.tensor, cols.offset, [list(cols.ap[0]), [HW, n], [1, OFFS], [1, HD]])


def build(nc, x, ctx_t, lat_down, lat_gb, lat_up, w_o, toep, gate_w, w_up, w_dn, out):
    x2_dram = nc.dram_tensor("x2_scratch", (B * S, D), F32).ap()
    x2_heads = x2_dram.rearrange("(b h i) d -> h b i d", b=B, h=HS)
    out_heads = out.rearrange("b (h i) d -> h b i d", h=HS)

    with ExitStack() as ctx:
        def sb(name, shape, dt=F32):
            return ctx.enter_context(nc.sbuf_tensor(name, shape, dt))

        def bank(name):
            return ctx.enter_context(nc.psum_tensor(name, [P, 512], F32))

        def sem(name):
            return ctx.enter_context(nc.semaphore(name))

        wu_hi = sb("wu_hi", [P, NW_UP], F32R)
        wu_lo = sb("wu_lo", [P, NW_UP], F32R)
        wd_hi = sb("wd_hi", [P, NW_DN], F32R)
        wd_lo = sb("wd_lo", [P, NW_DN], F32R)
        gw_hi = sb("gw_hi", [P, DC * E], F32R)
        gw_lo = sb("gw_lo", [P, DC * E], F32R)
        ident = sb("ident", [P, P])
        ident_b = sb("ident_b", [P, P], BF16)
        causal = sb("causal", [P, 4 * P], BF16)
        half_neg = sb("half_neg", [P, 2])
        eps = sb("eps", [P, 2])
        gb = sb("gb", [P, 2])
        with ExitStack() as lent:
            keys_split = lent.enter_context(nc.sbuf_tensor("keys_split", [P, 4 * 4 * P], F32R))
            queries_hi, queries_lo = [lent.enter_context(nc.sbuf_tensor(name, [P, 2, DC * P], F32R))
                                      for name in ("queries_hi", "queries_lo")]
        kv_hi = sb("kv_hi", [P, DC, B * PAIRS], F32R)
        t_hi = sb("t_hi", [P, 2 * P], F32R)
        t_lo = sb("t_lo", [P, 2 * P], F32R)
        hT_hi = sb("hT_hi", [P, 4, P], F32R)
        hT_lo = sb("hT_lo", [P, 4, P], F32R)
        kv_lo = sb("kv_lo", [P, DC, B * PAIRS], F32R)
        xT_hi = sb("xT_hi", [P, 2, DC, P], F32R)
        xT_lo = sb("xT_lo", [P, 2, DC, P], F32R)
        st = sb("st", [P, 2, 6])
        mv = sb("mv", [P, 2])
        ve = sb("ve", [P, 2])
        rstd = sb("rstd", [P, 2])
        mv2 = sb("mv2", [P, 2, 2])
        rstd2 = sb("rstd2", [P, 2])
        nmax = sb("nmax", [P, H])
        rden = sb("rden", [P, H])
        held = sb("held", [P, 1])
        g_max = sb("g_max", [P, 1])
        g_sum = sb("g_sum", [P, 2])
        euler = sb("euler", [P, 1])
        g_z = sb("g_z", [P, E])
        g_exp = sb("g_exp", [P, E])
        g_score = sb("g_score", [P, E + 8 - TOP])
        g_rest = sb("g_rest", [P, E + 8 - TOP])
        g_top = sb("g_top", [P, 8])
        g_sel = sb("g_sel", [P, E])
        comb = sb("comb", [P, 2, NE])

        scratch = sb("scratch", [P, SCRATCH])
        at = {"a": 0, "b": 0}

        def carve(stage, cols):
            first = at[stage]
            at[stage] += cols
            assert at[stage] <= SCRATCH
            return scratch[:, first:first + cols]

        stage_up = carve("a", SL_UP)
        stage_dn = carve("a", SL_DN)
        x_in = carve("a", D)
        xn = carve("a", D)
        xnT = carve("a", D)
        w_lat = carve("a", DC * 2 * LAT)
        lat_n = carve("a", 2 * LAT)
        latT = carve("a", P)
        probs = carve("a", 2 * 4 * P)
        probsT = carve("a", 2 * 4 * P)
        x_res = carve("a", D)
        vals = carve("a", H * (DH + 1)).rearrange("p (h c) -> p h c", h=H)
        att = carve("a", D)
        attT = carve("a", D)
        gw = attT[:, 0:DC * E]
        w_latup = carve("a", 4 * D)
        w_out = carve("a", DC * D)

        toep_in = carve("b", 2 * P + 1)
        ctx_in = carve("b", DC * B * HW)
        kv = carve("b", B * PAIRS)
        hid = carve("b", HCOLS)
        kv_first = hid[:, 0:B * PAIRS]
        assert SL_UP + SL_DN >= 2 * P + 1 + DC * B * HW
        mixed = carve("b", B // 2 * SLOTS * ZW)
        wrapped = carve("b", B // 2 * MIRROR).rearrange("p (b i) -> p b i", i=MIRROR)
        sil = carve("b", 3 * I)
        xq = carve("b", D)
        xqT = carve("b", DC * B * HW)
        x2_in = carve("b", D)
        conv_o = carve("b", D)
        x3 = [carve("b", D) for _ in range(2)]
        x3n = carve("b", D)

        banks = [bank(f"bank{i}") for i in range(8)]
        score_b = banks[0:4]
        front_b, qv_b, pv_b, proj_b = banks[4:8]
        up_b = banks[0:3]
        turn_b = banks[3]
        down_b = banks[4]
        conv_b = banks[5:7]
        misc_b = banks[7]

        w_lat_loaded = sem("w_lat_loaded")
        consts_loaded = sem("consts_loaded")
        blanks_made = sem("blanks_made")
        consts_made = sem("consts_made")
        gw_split = sem("gw_split")
        x_loaded = sem("x_loaded")
        xres_loaded = sem("xres_loaded")
        stage_loaded = sem("stage_loaded")
        weights_split = sem("weights_split")
        x_stats = sem("x_stats")
        x_rstd = sem("x_rstd")
        x_normed = sem("x_normed")
        xn_turned = sem("xn_turned")
        xnT_ready = sem("xnT_ready")
        lat_done = sem("lat_done")
        lat_stats = sem("lat_stats")
        lat_rstd = sem("lat_rstd")
        lat_normed = sem("lat_normed")
        lat_turned = sem("lat_turned")
        latT_ready = sem("latT_ready")
        k_done = sem("k_done")
        q_done = sem("q_done")
        q_taken = sem("q_taken")
        keys_zeroed = sem("keys_zeroed")
        k_hi_ready = sem("k_hi_ready")
        q_hi_ready = sem("q_hi_ready")
        k_taken = sem("k_taken")
        v_taken = sem("v_taken")
        scores_done = sem("scores_done")
        row_max = sem("row_max")
        exp_done = sem("exp_done")
        p_turned = sem("p_turned")
        pT_taken_v = sem("pT_taken_v")
        pT_taken_s = sem("pT_taken_s")
        weighed = sem("weighed")
        att_normed = sem("att_normed")
        att_turned = sem("att_turned")
        attT_ready = sem("attT_ready")
        proj_done = sem("proj_done")
        x2_made = sem("x2_made")
        x2_stored = sem("x2_stored")
        attn_vec = sem("attn_vec")
        attn_pool = sem("attn_pool")

        x2_loaded = sem("x2_loaded")
        ctx_loaded = sem("ctx_loaded")
        toep_loaded = sem("toep_loaded")
        q_stats = sem("q_stats")
        q_rstd = sem("q_rstd")
        q_normed = sem("q_normed")
        q_turned = sem("q_turned")
        qT_ready = sem("qT_ready")
        kv_made = sem("kv_made")
        kv_hi_ready = sem("kv_hi_ready")
        kv_lo_ready = sem("kv_lo_ready")
        toep_made = sem("toep_made")
        toep_hi_ready = sem("toep_hi_ready")
        toep_lo_ready = sem("toep_lo_ready")
        conv_done = sem("conv_done")
        conv_taken = sem("conv_taken")
        conv_summed = sem("conv_summed")
        conv_mixed = sem("conv_mixed")
        mixed_zeroed = sem("mixed_zeroed")
        conv_turned = sem("conv_turned")
        x3_made = sem("x3_made")
        x3_stats = sem("x3_stats")
        x3_rstd = sem("x3_rstd")
        x3_normed = sem("x3_normed")
        x3_turned = sem("x3_turned")
        xT_hi_ready = sem("xT_hi_ready")
        xT_lo_ready = sem("xT_lo_ready")
        gate_done = sem("gate_done")
        gate_max = sem("gate_max")
        gate_shifted = sem("gate_shifted")
        gate_exp = sem("gate_exp")
        up_done = sem("up_done")
        silu_done = sem("silu_done")
        h_made = sem("h_made")
        h_turned = sem("h_turned")
        hT_hi_ready = sem("hT_hi_ready")
        hT_lo_ready = sem("hT_lo_ready")
        down_read = sem("down_read")
        out_made = sem("out_made")
        out_stored = sem("out_stored")
        front_vec = sem("front_vec")
        front_pool = sem("front_pool")

        FRONT_LINKS = 13

        def hold(value):
            if not isinstance(value, int):
                nc.vector.memset(held[:, :], 0.0)

        def pair_products(eng, lc, dst):
            c = ctx_in[:, lc * B * HW:(lc + 1) * B * HW]
            once = c.rearrange("p (b i) -> p b i", b=B)[:, :, 0:HD].unsqueeze(2).broadcast_to([P, B, OFFS, HD])
            return eng.tensor_tensor(dst.rearrange("p (b d i) -> p b d i", b=B, d=OFFS), once, windows(c, B), ALU.mult)

        block = ctx.enter_context(nc.Block())

        def all_tiles(eng, tile):
            tile(fixed(0), None, fixed(1), fixed(2))
            with eng.Fori(0, (HS - 4) // 2) as k:
                for o in (1, 2):
                    tile(looped(k, o), looped(k, o - 1), looped(k, o + 1), looped(k, o + 2))
            tile(fixed(HS - 3), fixed(HS - 4), fixed(HS - 2), fixed(HS - 1))
            tile(fixed(HS - 2), fixed(HS - 3), fixed(HS - 1), None)
            tile(fixed(HS - 1), fixed(HS - 2), None, None)

        @block.sync
        def _(sp):
            def load_x(b):
                wait(sp, x_normed, b)
                sp.dma_start(x_in, x[b]).then_inc(x_loaded, 16)

            def load_stage(b):
                wait(sp, weights_split, b * 4)
                sp.dma_start(stage_up, w_up[:, bass.ds(b * SL_UP, SL_UP)]).then_inc(stage_loaded, 16)
                sp.dma_start(stage_dn, w_dn[:, bass.ds(b * SL_DN, SL_DN)]).then_inc(stage_loaded, 16)

            def load_res(b):
                wait(sp, x2_stored, b * 16)
                sp.dma_start(x_res, x[b]).then_inc(xres_loaded, 16)

            def store_x2(b):
                sp.wait_ge(x2_made, b + 1)
                sp.dma_start(x2_dram[bass.ds(b * S, S), :], x_res).then_inc(x2_stored, 16)

            load_x(0)
            sp.dma_start(w_lat, lat_down).then_inc(w_lat_loaded, 16)
            sp.dma_start(gb[:, :], lat_gb).then_inc(consts_loaded, 16)
            sp.dma_start(w_latup, lat_up).then_inc(consts_loaded, 16)
            sp.dma_start(w_out, w_o).then_inc(consts_loaded, 16)
            sp.dma_start(gw, gate_w).then_inc(consts_loaded, 16)
            load_stage(0)
            load_x(1)

            def batch(b, more):
                store_x2(b - 1)
                load_res(b)
                if more:
                    load_x(b + 3)
                load_stage(b + 2)

            load_res(0)
            load_stage(1)
            load_x(2)
            load_x(3)
            load_stage(2)
            with sp.Fori(1, B - 3) as b:
                batch(b, True)
            batch(B - 3, False)
            store_x2(B - 3)
            load_res(B - 2)

            def load_x2(t):
                wait(sp, x3_made, t.n)
                sp.dma_start(x2_in, x2_heads[t.n]).then_inc(x2_loaded, 16)

            def load_toep(t):
                wait(sp, toep_lo_ready, t.n)
                sp.dma_start(toep_in, toep[t.n]).then_inc(toep_loaded, 16)

            def load_ctx(t):
                wait(sp, kv_made, t.n * 2)
                sp.dma_start(ctx_in, ctx_t[t.n]).then_inc(ctx_loaded, 16)

            def store_out(t):
                sp.wait_ge(out_made, t.n + 1)
                sp.dma_start(out_heads[t.n], x3[t.p]).then_inc(out_stored, 16)

            sp.wait_ge(weights_split, 4 * B)
            load_toep(fixed(0))
            load_ctx(fixed(0))
            store_x2(B - 2)
            load_res(B - 1)
            load_ctx(fixed(1))
            load_toep(fixed(1))
            store_x2(B - 1)
            sp.wait_ge(x2_stored, 16 * B)
            load_x2(fixed(0))
            load_x2(fixed(1))
            load_ctx(fixed(2))

            def tile(t, prev, nxt, after):
                if after:
                    load_toep(after)
                if prev:
                    store_out(prev)
                if after:
                    load_x2(after)
                    if not (isinstance(after.n, int) and after.n == HS - 1):
                        load_ctx(later(after))

            all_tiles(sp, tile)
            store_out(fixed(HS - 1))
            sp.wait_ge(out_stored, 16 * HS)

        @block.gpsimd
        def _(pool):
            g = nc.gpsimd

            def rstd_x(b):
                pool.wait_ge(x_stats, b + 1)
                g.tensor_tensor(ve[:, 0:1], mv[:, 1:2], eps[:, 0:1], ALU.add).then_inc(attn_pool, 1)
                pool.wait_ge(attn_pool, b * 2 + 1)
                g.tensor_tensor(rstd[:, 0:1], ve[:, 0:1], half_neg[:, 0:1], ALU.pow).then_inc(x_rstd, 1)

            def rstd_lat(b):
                pool.wait_ge(x_rstd, b + 1)
                pool.wait_ge(lat_stats, b + 1)
                g.tensor_tensor(ve[:, :], mv2[:, :, 1], eps[:, :], ALU.add).then_inc(attn_pool, 1)
                pool.wait_ge(attn_pool, b * 2 + 2)
                g.tensor_tensor(rstd2[:, :], ve[:, :], half_neg[:, :], ALU.pow).then_inc(lat_rstd, 1)

            def split_up(b):
                pool.wait_ge(stage_loaded, b * 32 + 32)
                up = bass.ds(b * SL_UP, SL_UP)
                g.tensor_copy(wu_hi[:, up], stage_up).then_inc(weights_split, 1)
                pool.wait_ge(weights_split, b * 4 + 1)
                g.tensor_tensor(wu_lo[:, up], stage_up, wu_hi[:, up].bitcast(F32),
                                ALU.subtract).then_inc(weights_split, 1)

            def split_dn(b):
                dn = bass.ds(b * SL_DN, SL_DN)
                g.tensor_copy(wd_hi[:, dn], stage_dn).then_inc(weights_split, 1)
                pool.wait_ge(weights_split, b * 4 + 3)
                g.tensor_tensor(wd_lo[:, dn], stage_dn, wd_hi[:, dn].bitcast(F32),
                                ALU.subtract).then_inc(weights_split, 1)

            g.memset(half_neg[:, :], -0.5).then_inc(blanks_made, 1)
            g.memset(eps[:, :], EPS).then_inc(blanks_made, 1)
            g.memset(ident[:, :], 0.0).then_inc(blanks_made, 1)
            pool.wait_ge(blanks_made, 3)
            g.affine_select(out=ident[:, :], in_=ident[:, :], compare_op=ALU.not_equal, fill=1.0, base=0,
                            pattern=[[-1, P]], channel_multiplier=1).then_inc(consts_made, 1)
            g.memset(euler[:, :], math.e).then_inc(blanks_made, 1)
            g.memset(comb[:, :, E:NE], 1.0).then_inc(blanks_made, 1)
            g.memset(g_score[:, E:], -1.0).then_inc(blanks_made, 1)
            g.memset(vals[:, :, DH:DH + 1], 1.0).then_inc(blanks_made, 1)
            rstd_x(0)
            g.memset(ident_b[:, :], 0.0).then_inc(blanks_made, 1)
            g.memset(causal[:, :], 0.0).then_inc(blanks_made, 1)
            g.memset(keys_split[:, :].bitcast(F32), 0.0).then_inc(keys_zeroed, 1)
            pool.wait_ge(blanks_made, 9)
            g.affine_select(out=ident_b[:, :], in_=ident_b[:, :], compare_op=ALU.not_equal, fill=1.0, base=0,
                            pattern=[[-1, P]], channel_multiplier=1).then_inc(consts_made, 1)
            g.affine_select(out=causal[:, :].rearrange("p (h k) -> p h k", h=4),
                            in_=causal[:, :].rearrange("p (h k) -> p h k", h=4), compare_op=ALU.is_ge,
                            fill=MASKED, base=0, pattern=[[0, 4], [-1, P]],
                            channel_multiplier=1).then_inc(consts_made, 1)
            rstd_lat(0)
            g.memset(queries_lo[:, :, :].bitcast(F32), 0.0).then_inc(keys_zeroed, 1)
            rstd_x(1)
            pool.wait_ge(consts_loaded, 16 * 4)
            g.tensor_copy(gw_hi[:, :], gw).then_inc(gw_split, 1)
            pool.wait_ge(gw_split, 1)
            g.tensor_tensor(gw_lo[:, :], gw, gw_hi[:, :].bitcast(F32), ALU.subtract).then_inc(gw_split, 1)
            split_up(0)
            split_dn(0)
            with pool.Fori(0, B - 2) as b:
                rstd_lat(b + 1)
                rstd_x(b + 2)
                split_up(b + 1)
                split_dn(b + 1)
            rstd_lat(B - 1)
            split_up(B - 1)
            split_dn(B - 1)

            def rstd_of(t, stats, done):
                pool.wait_ge(stats, t.n + 1)
                g.tensor_tensor(ve[:, 0:1], mv[:, 1:2], eps[:, 0:1], ALU.add).then_inc(front_pool, 1)
                pool.wait_ge(front_pool, t.n * 2 + (1 if done is q_rstd else 2))
                g.tensor_tensor(rstd[:, 0:1], ve[:, 0:1], half_neg[:, 0:1], ALU.pow).then_inc(done, 1)

            def make_kv(t, lc):
                if lc == 0:
                    pool.wait_ge(ctx_loaded, t.n * 16 + 16)
                wait(pool, kv_lo_ready, t.n * 2 + lc)
                pair_products(g, lc, kv).then_inc(kv_made, 1)

            def kv_rest(t, lc):
                pool.wait_ge(kv_hi_ready, t.n * 2 + lc + 1)
                g.tensor_tensor(kv_lo[:, lc, :], kv, kv_hi[:, lc, :].bitcast(F32),
                                ALU.subtract).then_inc(kv_lo_ready, 1)

            def gate_exponent(t):
                pool.wait_ge(gate_shifted, t.n + 1)
                g.tensor_tensor(g_exp[:, :], euler[:, 0:1].broadcast_to([P, E]), g_z[:, :],
                                ALU.pow).then_inc(gate_exp, 1)

            def tile(t, prev, nxt, after):
                if after:
                    make_kv(after, 0)
                    kv_rest(after, 0)
                if nxt:
                    rstd_of(nxt, x3_stats, x3_rstd)
                if after:
                    make_kv(after, 1)
                    rstd_of(after, q_stats, q_rstd)
                if nxt:
                    gate_exponent(nxt)
                if after:
                    kv_rest(after, 1)

            make_kv(fixed(1), 0)
            rstd_of(fixed(0), q_stats, q_rstd)
            kv_rest(fixed(1), 0)
            rstd_of(fixed(0), x3_stats, x3_rstd)
            make_kv(fixed(1), 1)
            rstd_of(fixed(1), q_stats, q_rstd)
            gate_exponent(fixed(0))
            kv_rest(fixed(1), 1)
            all_tiles(pool, tile)

        @block.scalar
        def _(act):
            a = nc.scalar

            def take_xnT(b):
                act.wait_ge(xn_turned, b + 1)
                wait(act, lat_done, b)
                a.copy(xnT, front_b[:, 0:D]).then_inc(xnT_ready, 1)

            def take_latT(b):
                act.wait_ge(lat_turned, b + 1)
                a.activation(latT, front_b[:, 3 * P:4 * P], ACT.Identity, bias=gb[:, 1:2],
                             scale=gb[:, 0:1]).then_inc(latT_ready, 1)

            def round_q(b, p):
                if p == 0:
                    act.wait_ge(q_done, b + 1)
                    wait(act, scores_done, b * 4)
                rows = slice(64 * p, 64 * p + 64)
                for q in range(2):
                    ins = a.activation(queries_hi[64 * q:64 * q + 64, p, :], qv_b[rows, 0:D], ACT.Copy,
                                       scale=float(DH) ** -0.5)
                ins.then_inc(q_hi_ready, 1)

            def round_k(b, r):
                if r == 0:
                    act.wait_ge(k_done, b + 1)
                rows, block = slice(32 * r, 32 * r + 32), slice(4 * P * r, 4 * P * (r + 1))
                a.copy(keys_split[rows, block], front_b[rows, :]).then_inc(k_hi_ready, 1)

            def round_qk(b):
                for p in range(2):
                    round_q(b, p)
                    round_k(b, 2 * p)
                    round_k(b, 2 * p + 1)

            def exps(b, r):
                act.wait_ge(row_max, b * 4 + r + 1)
                wait(act, p_turned, b * 4 + r - 1)
                for s in range(4 * r, 4 * r + 4):
                    ins = a.activation(probs[:, (s % 8) * P:(s % 8 + 1) * P],
                                       score_b[r][:, (s % 4) * P:(s % 4 + 1) * P],
                                       ACT.Exp, bias=nmax[:, s:s + 1])
                ins.then_inc(exp_done, 1)

            def take_attT(b):
                act.wait_ge(att_turned, b + 1)
                a.copy(attT, proj_b[:, 0:D]).then_inc(attT_ready, 1)

            def batch(b, n1, n2):
                if isinstance(b, int) and b == 0:
                    act.wait_ge(gw_split, 2)
                else:
                    take_attT(b - 1)
                exps(b, 2)
                exps(b, 3)
                if n1 is not None:
                    take_latT(n1)
                    round_qk(n1)
                act.wait_ge(p_turned, b * 4 + 4)
                act.wait_ge(weighed, b * 4 + 2)
                a.copy(probsT[:, 4 * P:8 * P], score_b[3][:, :]).then_inc(pT_taken_s, 1)
                if n1 is not None:
                    exps(n1, 0)
                if n2 is not None:
                    take_xnT(n2)
                if n1 is not None:
                    exps(n1, 1)

            take_xnT(0)
            act.wait_ge(consts_loaded, 16 * 4)
            take_latT(0)
            act.wait_ge(keys_zeroed, 1)
            round_qk(0)
            exps(0, 0)
            exps(0, 1)
            take_xnT(1)
            batch(0, 1, 2)
            with act.Fori(1, B - 2) as b:
                batch(b, b + 1, b + 2)
            batch(B - 2, B - 1, None)
            batch(B - 1, None, None)

            def kv_round(t, lc):
                act.wait_ge(kv_made, t.n * 2 + lc + 1)
                wait(act, conv_done, t.n * 4)
                src = kv_first if isinstance(t.n, int) and t.n == 0 and lc == 1 else kv
                a.copy(kv_hi[:, lc, :], src).then_inc(kv_hi_ready, 1)

            def take_qT(t):
                act.wait_ge(q_turned, t.n + 1)
                wait(act, conv_mixed, t.n * 4)
                src = misc_b[:, 0:D].rearrange("p (g i) -> p g i", i=HD)
                dst = xqT.rearrange("p (g i) -> p g i", i=HW)
                a.copy(dst[:, :, 0:HD], src)
                a.copy(dst[:, :, HD:HW], src[:, :, 0:HW - HD]).then_inc(qT_ready, 1)

            def toep_round(t):
                act.wait_ge(toep_made, t.n + 1)
                wait(act, conv_done, t.n * 4)
                a.copy(t_hi[:, :], toep_in[:, 0:2 * P]).then_inc(toep_hi_ready, 1)

            def x3T_round(t):
                act.wait_ge(x3_turned, t.n + 1)
                a.copy(xT_hi[:, t.p, :, :], misc_b[:, 0:D].rearrange("p (c n) -> p c n", c=DC)).then_inc(xT_hi_ready, 1)

            def silu(t, e):
                act.wait_ge(up_done, t.n * NE + e + 1)
                a.activation(sil[:, (e % 3) * I:(e % 3 + 1) * I], up_b[e % 3][:, 0:I], ACT.Silu).then_inc(silu_done, 1)

            def h_round(t, grp):
                act.wait_ge(h_turned, t.n * NG + grp + 1)
                wait(act, down_read, t.n * NG + grp)
                n = min(4, NCH - 4 * grp)
                rows = P if grp < NG - 1 else LAST
                a.copy(hT_hi[0:rows, 0:n, :],
                       turn_b[0:rows, 0:n * P].rearrange("p (c n) -> p c n", c=n)).then_inc(hT_hi_ready, 1)

            def tile(t, prev, nxt, after):
                for e in range(NE):
                    silu(t, e)
                    for grp, s in TAIL_TURN_AT.items():
                        if prev and s == e:
                            h_round(prev, grp)
                    for grp, s in TURN_AT.items():
                        if s == e:
                            h_round(t, grp)
                    if nxt and e == 1:
                        take_qT(nxt)
                    if after and e == 7:
                        kv_round(after, 0)
                    if after and e == 10:
                        toep_round(after)
                    if nxt and e == 12:
                        x3T_round(nxt)
                    if after and e == 13:
                        kv_round(after, 1)

            toep_round(fixed(0))
            kv_round(fixed(0), 0)
            kv_round(fixed(0), 1)
            take_attT(B - 1)
            take_qT(fixed(0))
            kv_round(fixed(1), 0)
            toep_round(fixed(1))
            x3T_round(fixed(0))
            kv_round(fixed(1), 1)
            all_tiles(act, tile)
            h_round(fixed(HS - 1), 5)
            h_round(fixed(HS - 1), 6)

        @block.vector
        def _(dve):
            v = nc.vector

            def x_statistics(b):
                dve.wait_ge(x_loaded, b * 16 + 16)
                v.bn_stats(st[:, 0, :], x_in).then_inc(attn_vec, 1)
                dve.wait_ge(attn_vec, {0: 1, 1: 3}[b] if isinstance(b, int) and b < 2 else b * 3 - 1)
                hold(b)
                v.bn_aggr(mv[:, :], st[:, 0, :]).then_inc(x_stats, 1)

            def norm_x(b):
                dve.wait_ge(x_rstd, b + 1)
                wait(dve, xn_turned, b)
                v.tensor_scalar(xn, x_in, mv[:, 0:1], rstd[:, 0:1], ALU.subtract, ALU.mult).then_inc(x_normed, 1)

            def lat_statistics(b):
                dve.wait_ge(lat_done, b + 1)
                for i in range(2):
                    ins = v.bn_stats(st[:, i, :], front_b[:, 2 * P + i * LAT:2 * P + (i + 1) * LAT])
                ins.then_inc(attn_vec, 1)
                dve.wait_ge(attn_vec, 2 if isinstance(b, int) and b == 0 else b * 3 + 1)
                hold(b)
                for i in range(2):
                    ins = v.bn_aggr(mv2[:, i, :], st[:, i, :])
                ins.then_inc(lat_stats, 1)

            def norm_lat(b):
                dve.wait_ge(lat_rstd, b + 1)
                wait(dve, lat_turned, b)
                for i in range(2):
                    ins = v.tensor_scalar(lat_n[:, i * LAT:(i + 1) * LAT],
                                          front_b[:, 2 * P + i * LAT:2 * P + (i + 1) * LAT],
                                          mv2[:, i, 0:1], rstd2[:, i:i + 1], ALU.subtract, ALU.mult)
                ins.then_inc(lat_normed, 1)

            def rest_q(b, p):
                dve.wait_ge(q_hi_ready, b * 2 + p + 1)
                rows = slice(64 * p, 64 * p + 64)
                v.scalar_tensor_tensor(out=queries_lo[rows, p, :], in0=qv_b[rows, 0:D], scalar=float(DH) ** -0.5,
                                       in1=queries_hi[rows, p, :].bitcast(F32), op0=ALU.mult,
                                       op1=ALU.subtract).then_inc(q_taken, 1)

            def rest_k(b, r):
                dve.wait_ge(k_hi_ready, b * 4 + r + 1)
                rows, block = slice(32 * r, 32 * r + 32), slice(4 * P * r, 4 * P * (r + 1))
                further = (32 * r + P // 2) % P
                v.tensor_tensor(keys_split[further:further + 32, block], front_b[rows, :],
                                keys_split[rows, block].bitcast(F32), ALU.subtract).then_inc(k_taken, 1)

            def rest_qk(b):
                for p in range(2):
                    rest_q(b, p)
                    rest_k(b, 2 * p)
                    rest_k(b, 2 * p + 1)

            def take_v(b):
                wait(dve, weighed, b * 4)
                v.tensor_copy(vals[:, :, 0:DH],
                              qv_b[:, D:2 * D].rearrange("p (h c) -> p h c", h=H)).then_inc(v_taken, 1)

            def take_pT(b, r):
                dve.wait_ge(p_turned, b * 4 + r + 1)
                wait(dve, weighed, b * 4 + r - 1)
                v.tensor_copy(probsT[:, (r % 2) * 4 * P:(r % 2 + 1) * 4 * P], score_b[r][:, :]).then_inc(pT_taken_v, 1)

            def row_maxima(b):
                for r in range(4):
                    dve.wait_ge(scores_done, b * 4 + r + 1)
                    wait(dve, exp_done, b * 4 + r - 3)
                    v.tensor_reduce(nmax[:, 4 * r:4 * r + 4], score_b[r][:, :].rearrange("p (h k) -> p h k", h=4),
                                    AX_X, ALU.max, negate=True).then_inc(row_max, 1)

            def take_proj(b):
                dve.wait_ge(proj_done, b + 1)
                dve.wait_ge(xres_loaded, b * 16 + 16)
                v.tensor_tensor(x_res, proj_b[:, D:2 * D], x_res, ALU.add).then_inc(x2_made, 1)

            def norm_att(b, links):
                dve.wait_ge(weighed, b * 4 + 4)
                o = pv_b[:, 0:H * (DH + 1)].rearrange("p (h c) -> p h c", h=H)
                v.reciprocal(rden[:, :], o[:, :, DH]).then_inc(attn_vec, 1)
                dve.wait_ge(attn_vec, links)
                wait(dve, att_turned, b)
                v.tensor_tensor(att.rearrange("p (h c) -> p h c", h=H), o[:, :, 0:DH],
                                rden[:, :].unsqueeze(2).broadcast_to([P, H, DH]), ALU.mult).then_inc(att_normed, 1)

            def batch(b, n1, n2):
                before = not isinstance(b, int) or b > 0
                if before:
                    norm_att(b - 1, b * 3 + (3 if n1 is not None else 2))
                take_v(b)
                if n1 is not None:
                    lat_statistics(n1)
                take_pT(b, 0)
                take_pT(b, 1)
                if n1 is not None:
                    norm_lat(n1)
                if n2 is not None:
                    x_statistics(n2)
                if before:
                    take_proj(b - 1)
                take_pT(b, 2)
                if n2 is not None:
                    norm_x(n2)
                if n1 is not None:
                    rest_qk(n1)
                if n1 is not None:
                    row_maxima(n1)

            x_statistics(0)
            norm_x(0)
            lat_statistics(0)
            norm_lat(0)
            x_statistics(1)
            norm_x(1)
            dve.wait_ge(keys_zeroed, 2)
            rest_qk(0)
            row_maxima(0)
            batch(0, 1, 2)
            with dve.Fori(1, B - 2) as b:
                batch(b, b + 1, b + 2)
            batch(B - 2, B - 1, None)
            batch(B - 1, None, None)

            def statistics(src, done, chain):
                chain.link(v.bn_stats(st[:, 0, :], src))
                hold(chain.base)
                v.bn_aggr(mv[:, :], st[:, 0, :]).then_inc(done, 1)

            def q_statistics(t, chain):
                dve.wait_ge(x2_loaded, t.n * 16 + 16)
                statistics(x2_in, q_stats, chain)

            def norm_q(t):
                dve.wait_ge(q_rstd, t.n + 1)
                v.tensor_scalar(xq, x2_in, mv[:, 0:1], rstd[:, 0:1], ALU.subtract, ALU.mult).then_inc(q_normed, 1)

            def toep_diag(t):
                w = toep_in
                dve.wait_ge(toep_loaded, t.n * 16 + 16)
                v.scalar_tensor_tensor(out=w[:, 0:P], in0=ident[:, :], scalar=w[:, 2 * P:2 * P + 1], in1=w[:, 0:P],
                                       op0=ALU.mult, op1=ALU.add).then_inc(toep_made, 1)

            def toep_rest(t):
                dve.wait_ge(toep_hi_ready, t.n + 1)
                v.tensor_tensor(t_lo[:, :], toep_in[:, 0:2 * P], t_hi[:, :].bitcast(F32),
                                ALU.subtract).then_inc(toep_lo_ready, 1)

            def mix(t, u):
                lc, n = divmod(u, 2)
                if u == 0:
                    dve.wait_ge(qT_ready, t.n + 1)
                dve.wait_ge(conv_done, t.n * 4 + u + 1)
                wait(dve, conv_mixed, t.n * 4 + u)
                nb = B // 2
                first = (lc * B + n * nb) * HW
                q = xqT[:, first:first + nb * HW]
                y = conv_b[u % 2][:, 0:HALF].rearrange("p (b d i) -> p b d i", b=nb, d=OFFS)
                z = mixed.rearrange("p (b s i) -> p b s i", b=nb, s=SLOTS)
                v.tensor_tensor(z[:, :, 0:OFFS, 0:HD], y, windows(q, nb), ALU.mult)
                ahead = bass.AP(mixed.tensor, mixed.offset + OFFS * ZW + 1,
                                [list(mixed.ap[0]), [SLOTS * ZW, nb], [ZW + 1, MIRROR], [1, HD]])
                once = q.rearrange("p (b i) -> p b i", b=nb)[:, :, 0:HD].unsqueeze(2)
                v.tensor_tensor(ahead, y[:, :, 1:1 + MIRROR, :], once.broadcast_to([P, nb, MIRROR, HD]),
                                ALU.mult).then_inc(conv_taken, 1)
                dve.wait_ge(conv_taken, t.n * 4 + u + 1)
                by_channel = mixed.rearrange("p (b s i) -> p b i s", b=nb, s=SLOTS)
                o = conv_o[:, lc * P + n * 64:lc * P + (n + 1) * 64].rearrange("p (b i) -> p b i", b=nb)
                v.tensor_reduce(o, by_channel[:, :, 0:HD, :], AX_X, ALU.add)
                v.tensor_reduce(wrapped, by_channel[:, :, HD:ZW, OFFS:SLOTS], AX_X, ALU.add).then_inc(conv_summed, 1)
                dve.wait_ge(conv_summed, t.n * 4 + u + 1)
                v.tensor_tensor(o[:, :, 0:MIRROR], o[:, :, 0:MIRROR], wrapped, ALU.add).then_inc(conv_mixed, 1)

            def make_x3(t, chain):
                dve.wait_ge(conv_turned, t.n + 1)
                wait(dve, out_stored, t.n * 16 - 16)
                v.tensor_tensor(x3[t.p], misc_b[:, 0:D], x2_in, ALU.add).then_inc(x3_made, 1)
                dve.wait_ge(x3_made, t.n + 1)
                statistics(x3[t.p], x3_stats, chain)

            def norm_x3(t):
                dve.wait_ge(x3_rstd, t.n + 1)
                v.tensor_scalar(x3n, x3[t.p], mv[:, 0:1], rstd[:, 0:1], ALU.subtract, ALU.mult).then_inc(x3_normed, 1)

            def x3T_rest(t):
                dve.wait_ge(xT_hi_ready, t.n + 1)
                v.tensor_tensor(xT_lo[:, t.p, :, :], misc_b[:, 0:D].rearrange("p (c n) -> p c n", c=DC),
                                xT_hi[:, t.p, :, :].bitcast(F32), ALU.subtract).then_inc(xT_lo_ready, 1)

            def gate_maximum(t):
                dve.wait_ge(gate_done, t.n + 1)
                v.tensor_reduce(g_max[:, :], misc_b[:, D:D + E], AX_X, ALU.max, negate=True).then_inc(gate_max, 1)
                dve.wait_ge(gate_max, t.n + 1)
                v.tensor_tensor(g_z[:, :], misc_b[:, D:D + E], g_max[:, 0:1].broadcast_to([P, E]),
                                ALU.add).then_inc(gate_shifted, 1)

            def gate_top(t, chain):
                dve.wait_ge(gate_exp, t.n + 1)
                chain.link(v.reduce_sum(g_sum[:, 0:1], g_exp[:, :], AX_X))
                chain.link(v.reciprocal(g_sum[:, 1:2], g_sum[:, 0:1]))
                chain.link(v.tensor_scalar(g_score[:, 0:E], g_exp[:, :], g_sum[:, 1:2], None, ALU.mult))
                hold(chain.base)
                chain.link(v.max(g_top[:, :], g_score[:, 0:E]))
                chain.link(v.memset(g_top[:, TOP:8], -1.0))

            def gate_weights(t, chain):
                hold(chain.base)
                chain.link(v.match_replace(g_rest[:, :], g_top[:, :], g_score[:, :], 0.0))
                chain.link(v.tensor_tensor(g_sel[:, :], g_score[:, 0:E], g_rest[:, 0:E], ALU.subtract))
                chain.link(v.reduce_sum(g_sum[:, 0:1], g_sel[:, :], AX_X))
                chain.link(v.tensor_scalar(g_sum[:, 0:1], g_sum[:, 0:1], 1e-20, None, ALU.add))
                chain.link(v.reciprocal(g_sum[:, 1:2], g_sum[:, 0:1]))
                chain.link(v.tensor_scalar(comb[:, t.p, 0:E], g_sel[:, :], g_sum[:, 1:2], None, ALU.mult))

            def hidden(t, e):
                dve.wait_ge(silu_done, t.n * NE + e + 1)
                grp = (I * (e + 1) - 1) // 512
                wait(dve, h_turned, t.n * NG - NG + grp + 1)
                v.scalar_tensor_tensor(out=hid[:, e * I:(e + 1) * I], in0=sil[:, (e % 3) * I:(e % 3 + 1) * I],
                                       scalar=comb[:, t.p, e:e + 1], in1=up_b[e % 3][:, I:2 * I],
                                       op0=ALU.mult, op1=ALU.mult).then_inc(h_made, 1)

            def h_rest(t, grp):
                dve.wait_ge(hT_hi_ready, t.n * NG + grp + 1)
                n = min(4, NCH - 4 * grp)
                rows = P if grp < NG - 1 else LAST
                v.tensor_tensor(hT_lo[0:rows, 0:n, :], turn_b[0:rows, 0:n * P].rearrange("p (c n) -> p c n", c=n),
                                hT_hi[0:rows, 0:n, :].bitcast(F32), ALU.subtract).then_inc(hT_lo_ready, 1)

            def finish(t):
                dve.wait_ge(down_read, t.n * NG + NG)
                v.tensor_tensor(x3[t.p], down_b[:, 0:D], x3[t.p], ALU.add).then_inc(out_made, 1)

            def tile(t, prev, nxt, after):
                chain = Chain(dve, front_vec, nxt.n * FRONT_LINKS + 1) if nxt else None
                for e in range(NE):
                    hidden(t, e)
                    for grp, s in TAIL_TURN_AT.items():
                        if prev and s == e:
                            h_rest(prev, grp)
                    for grp, s in TURN_AT.items():
                        if s == e:
                            h_rest(t, grp)
                    if prev and e == 6:
                        finish(prev)
                    for u, s in MIX_AT.items():
                        if nxt and s == e:
                            mix(nxt, u)
                    if nxt and e == 9:
                        make_x3(nxt, chain)
                    if nxt and e == 10:
                        norm_x3(nxt)
                    if after and e == 9:
                        toep_diag(after)
                    if after and e == 11:
                        toep_rest(after)
                    if nxt and e == 12:
                        x3T_rest(nxt)
                    if after and e == 13:
                        q_statistics(after, chain)
                    if nxt and e == 14:
                        gate_maximum(nxt)
                    if after and e == 14:
                        norm_q(after)
                    if nxt and e == 16:
                        gate_top(nxt, chain)
                    if nxt and e == 17:
                        gate_weights(nxt, chain)
                        chain.close(FRONT_LINKS if after else FRONT_LINKS - 1)

            def first_kv_rest(lc, src):
                dve.wait_ge(kv_hi_ready, lc + 1)
                v.tensor_tensor(kv_lo[:, lc, :], src, kv_hi[:, lc, :].bitcast(F32),
                                ALU.subtract).then_inc(kv_lo_ready, 1)

            dve.wait_ge(consts_made, 3)
            t0, t1 = fixed(0), fixed(1)
            toep_diag(t0)
            dve.wait_ge(ctx_loaded, 16)
            pair_products(v, 0, kv).then_inc(kv_made, 1)
            pair_products(v, 1, kv_first).then_inc(kv_made, 1)
            norm_att(B - 1, B * 3)
            first_kv_rest(0, kv)
            first_kv_rest(1, kv_first)
            toep_rest(t0)
            take_proj(B - 1)

            chain = Chain(dve, front_vec, 0)
            q_statistics(t0, chain)
            norm_q(t0)
            chain.close(1)
            v.memset(mixed, 0.0).then_inc(mixed_zeroed, 1)
            dve.wait_ge(mixed_zeroed, 1)
            for u in range(4):
                mix(t0, u)
            chain = Chain(dve, front_vec, 1)
            make_x3(t0, chain)
            toep_diag(t1)
            norm_x3(t0)
            toep_rest(t1)
            x3T_rest(t0)
            q_statistics(t1, chain)
            gate_maximum(t0)
            norm_q(t1)
            gate_top(t0, chain)
            gate_weights(t0, chain)
            chain.close(FRONT_LINKS)
            all_tiles(dve, tile)
            h_rest(fixed(HS - 1), 5)
            h_rest(fixed(HS - 1), 6)
            finish(fixed(HS - 1))

        @block.tensor
        def _(pe):
            mm = nc.tensor.matmul

            def three(out_ap, stat, mov, first, last):
                (s_hi, s_lo), (m_hi, m_lo) = stat, mov
                mm(out_ap, s_hi, m_hi, start=first, stop=False, skip_group_check=True)
                mm(out_ap, s_hi, m_lo, start=False, stop=False, skip_group_check=True)
                return mm(out_ap, s_lo, m_hi, start=False, stop=last, skip_group_check=True)

            def turn_x(b):
                pe.wait_ge(x_normed, b + 1)
                wait(pe, k_taken, b * 4)
                for c in range(DC):
                    ins = nc.tensor.transpose(front_b[:, c * P:(c + 1) * P], xn[:, c * P:(c + 1) * P], ident[:, :])
                ins.then_inc(xn_turned, 1)

            def latents(b):
                pe.wait_ge(xnT_ready, b + 1)
                for c in range(DC):
                    ins = mm(front_b[:, 2 * P:3 * P], xnT[:, c * P:(c + 1) * P], w_lat[:, c * P:(c + 1) * P],
                             start=(c == 0), stop=(c == DC - 1))
                ins.then_inc(lat_done, 1)

            def turn_lat(b):
                pe.wait_ge(lat_normed, b + 1)
                nc.tensor.transpose(front_b[:, 3 * P:4 * P], lat_n, ident[:, :]).then_inc(lat_turned, 1)

            def keys(b):
                pe.wait_ge(latT_ready, b + 1)
                for slot in range(2 * DC):
                    ins = mm(front_b[:, slot * P:(slot + 1) * P], w_latup[:, 2 * D + slot * P:2 * D + (slot + 1) * P],
                             latT, start=True, stop=True)
                ins.then_inc(k_done, 1)

            def values(b):
                pe.wait_ge(latT_ready, b + 1)
                wait(pe, q_taken, b * 2)
                wait(pe, v_taken, b)
                mm(qv_b[:, D:2 * D], latT, w_latup[:, D:2 * D], start=True, stop=True)

            def queries(b):
                for c in range(DC):
                    ins = mm(qv_b[:, c * P:(c + 1) * P], w_latup[:, c * P:(c + 1) * P], latT, start=True, stop=True)
                ins.then_inc(q_done, 1)

            def scores(b, r):
                pe.wait_ge(q_taken, b * 2 + r // 2 + 1)
                pe.wait_ge(k_taken, b * 4 + r + 1)
                if r < 3:
                    wait(pe, pT_taken_v, b * 3 - 2 + r)
                else:
                    wait(pe, pT_taken_s, b)
                mm(score_b[r][:, :], ident_b[:, :], causal[:, :], start=True, stop=False, skip_group_check=True)
                for c in range(DC):
                    o = 2 * c * P
                    q, k = slice(c * P, (c + 1) * P), slice(4 * P * r + o, 4 * P * r + o + 2 * P)
                    for part in (queries_hi, queries_lo):
                        ins = mm(score_b[r][:, o:o + 2 * P], part[:, r // 2, q], keys_split[:, k], start=False,
                                 stop=(c == 1 and part is queries_lo), skip_group_check=True)
                ins.then_inc(scores_done, 1)

            def turn_p(b, r):
                pe.wait_ge(exp_done, b * 4 + r + 1)
                for s in range(4):
                    ins = nc.tensor.transpose(score_b[r][:, s * P:(s + 1) * P],
                                              probs[:, (4 * (r % 2) + s) * P:(4 * (r % 2) + s + 1) * P], ident[:, :])
                ins.then_inc(p_turned, 1)

            def weigh(b, r):
                if r == 0:
                    pe.wait_ge(v_taken, b + 1)
                    wait(pe, att_normed, b)
                if r < 3:
                    pe.wait_ge(pT_taken_v, b * 3 + r + 1)
                else:
                    pe.wait_ge(pT_taken_s, b + 1)
                for s in range(4):
                    h = 8 * (s // 2) + 2 * r + s % 2
                    o = h * (DH + 1)
                    q = (4 * (r % 2) + s) * P
                    ins = mm(pv_b[:, o:o + DH + 1], probsT[:, q:q + P], vals[:, h, :], start=True, stop=True)
                ins.then_inc(weighed, 1)

            def project_turn(b):
                pe.wait_ge(att_normed, b + 1)
                wait(pe, x2_made, b)
                for c in range(DC):
                    ins = nc.tensor.transpose(proj_b[:, c * P:(c + 1) * P], att[:, c * P:(c + 1) * P], ident[:, :])
                ins.then_inc(att_turned, 1)

            def project(b):
                pe.wait_ge(attT_ready, b + 1)
                for c in range(DC):
                    ins = mm(proj_b[:, D:2 * D], attT[:, c * P:(c + 1) * P], w_out[:, c * D:(c + 1) * D],
                             start=(c == 0), stop=(c == DC - 1))
                ins.then_inc(proj_done, 1)

            def batch(b, n1, n2):
                before = not isinstance(b, int) or b > 0
                turn_p(b, 0)
                if n1 is not None:
                    latents(n1)
                if before:
                    project_turn(b - 1)
                turn_p(b, 1)
                if before:
                    project(b - 1)
                weigh(b, 0)
                if n1 is not None:
                    turn_lat(n1)
                turn_p(b, 2)
                if n1 is not None:
                    values(n1)
                    queries(n1)
                    keys(n1)
                weigh(b, 1)
                turn_p(b, 3)
                if n1 is not None:
                    scores(n1, 0)
                    scores(n1, 1)
                weigh(b, 2)
                if n1 is not None:
                    scores(n1, 2)
                    scores(n1, 3)
                if n2 is not None:
                    turn_x(n2)
                weigh(b, 3)

            pe.wait_ge(consts_made, 1)
            turn_x(0)
            pe.wait_ge(w_lat_loaded, 16)
            latents(0)
            turn_lat(0)
            pe.wait_ge(consts_loaded, 16 * 4)
            pe.wait_ge(consts_made, 3)
            values(0)
            queries(0)
            keys(0)
            for r in range(4):
                scores(0, r)
            turn_x(1)
            batch(0, 1, 2)
            with pe.Fori(1, B - 2) as b:
                batch(b, b + 1, b + 2)
            batch(B - 2, B - 1, None)
            batch(B - 1, None, None)
            project_turn(B - 1)
            project(B - 1)

            def turn_q(t):
                pe.wait_ge(q_normed, t.n + 1)
                wait(pe, gate_shifted, t.n)
                for c in range(DC):
                    ins = nc.tensor.transpose(misc_b[:, c * P:(c + 1) * P], xq[:, c * P:(c + 1) * P], ident[:, :])
                ins.then_inc(q_turned, 1)

            def conv(t, u):
                lc, n = divmod(u, 2)
                if u == 0:
                    pe.wait_ge(toep_lo_ready, t.n + 1)
                    pe.wait_ge(kv_lo_ready, t.n * 2 + 2)
                wait(pe, conv_taken, t.n * 4 + u - 1)
                cols = slice(n * HALF, (n + 1) * HALF)
                for mc in range(lc + 1):
                    tap = slice((lc - mc) * P, (lc - mc + 1) * P)
                    ins = three(conv_b[u % 2][:, 0:HALF], (t_hi[:, tap], t_lo[:, tap]),
                                (kv_hi[:, mc, cols], kv_lo[:, mc, cols]), mc == 0, mc == lc)
                ins.then_inc(conv_done, 1)

            def turn_conv(t):
                pe.wait_ge(conv_mixed, t.n * 4 + 4)
                pe.wait_ge(qT_ready, t.n + 1)
                for c in range(DC):
                    ins = nc.tensor.transpose(misc_b[:, c * P:(c + 1) * P], conv_o[:, c * P:(c + 1) * P], ident[:, :])
                ins.then_inc(conv_turned, 1)

            def turn_x3(t):
                pe.wait_ge(x3_normed, t.n + 1)
                for c in range(DC):
                    ins = nc.tensor.transpose(misc_b[:, c * P:(c + 1) * P], x3n[:, c * P:(c + 1) * P], ident[:, :])
                ins.then_inc(x3_turned, 1)

            def gate(t):
                pe.wait_ge(xT_lo_ready, t.n + 1)
                for c in range(DC):
                    ins = three(misc_b[:, D:D + E], (xT_hi[:, t.p, c, :], xT_lo[:, t.p, c, :]),
                                (gw_hi[:, c * E:(c + 1) * E], gw_lo[:, c * E:(c + 1) * E]), c == 0, c == DC - 1)
                ins.then_inc(gate_done, 1)

            def up(t, e):
                if e == 0:
                    pe.wait_ge(xT_lo_ready, t.n + 1)
                wait(pe, h_made, t.n * NE + e - 2)
                for c in range(DC):
                    o = (c * NE + e) * UC
                    ins = three(up_b[e % 3][:, 0:UC], (xT_hi[:, t.p, c, :], xT_lo[:, t.p, c, :]),
                                (wu_hi[:, o:o + UC], wu_lo[:, o:o + UC]), c == 0, c == DC - 1)
                ins.then_inc(up_done, 1)

            def turn_h(t, grp):
                last_expert = (min(512 * (grp + 1), HCOLS) - 1) // I
                pe.wait_ge(h_made, t.n * NE + last_expert + 1)
                wait(pe, hT_lo_ready, t.n * NG + grp)
                for j in range(4 * grp, min(4 * grp + 4, NCH)):
                    rows = P if j < NCH - 1 else LAST
                    ins = nc.tensor.transpose(turn_b[0:rows, (j % 4) * P:(j % 4 + 1) * P], hid[:, j * P:j * P + rows],
                                              ident[:, :])
                ins.then_inc(h_turned, 1)

            def down(t, grp):
                pe.wait_ge(hT_lo_ready, t.n * NG + grp + 1)
                if grp == 0:
                    wait(pe, out_made, t.n)
                for j in range(4 * grp, min(4 * grp + 4, NCH)):
                    rows = P if j < NCH - 1 else LAST
                    ins = three(down_b[:, 0:D], (hT_hi[0:rows, j % 4, :], hT_lo[0:rows, j % 4, :]),
                                (wd_hi[0:rows, j * D:(j + 1) * D], wd_lo[0:rows, j * D:(j + 1) * D]),
                                j == 0, j == NCH - 1)
                ins.then_inc(down_read, 1)

            def tile(t, prev, nxt, after):
                for e in range(NE):
                    up(t, e)
                    for grp, s in TAIL_DOWN_AT.items():
                        if prev and s == e:
                            down(prev, grp)
                    for grp, s in DOWN_AT.items():
                        if s == e:
                            down(t, grp)
                    if nxt and e == 1:
                        turn_q(nxt)
                    for grp, s in TAIL_TURN_AT.items():
                        if prev and s == e:
                            turn_h(prev, grp)
                    for grp, s in TURN_AT.items():
                        if s == e:
                            turn_h(t, grp)
                    for u, s in CONV_AT.items():
                        if nxt and s == e:
                            conv(nxt, u)
                    if nxt and e == 9:
                        turn_conv(nxt)
                    if nxt and e == 12:
                        turn_x3(nxt)
                    if nxt and e == 13:
                        gate(nxt)

            pe.wait_ge(gw_split, 2)
            t0 = fixed(0)
            conv(t0, 0)
            conv(t0, 1)
            turn_q(t0)
            conv(t0, 2)
            conv(t0, 3)
            turn_conv(t0)
            turn_x3(t0)
            gate(t0)
            pe.wait_ge(weights_split, 4 * B)
            all_tiles(pe, tile)
            end = fixed(HS - 1)
            down(end, 4)
            turn_h(end, 5)
            down(end, 5)
            turn_h(end, 6)
            down(end, 6)


def kernel(x, ctx_2048, L0_attn_W_dq, L0_attn_W_uq, L0_attn_q_ln_g, L0_attn_q_ln_b, L0_attn_W_dkv, L0_attn_W_ukv,
           L0_attn_kv_ln_g, L0_attn_kv_ln_b, L0_attn_W_o, L0_xattn_ssm_kernel, L0_xattn_D, L0_ffn_gate_w,
           L0_ffn_w13, L0_ffn_w2, L0_ffn_sw13, L0_ffn_sw2):
    import numpy as np
    import concourse.bacc as bacc
    from concourse.bass_utils import run_bass_kernel_spmd

    f = np.float32
    a = {k: np.asarray(w) for k, w in dict(
        x=x, ctx=ctx_2048, wdq=L0_attn_W_dq, wuq=L0_attn_W_uq, qg=L0_attn_q_ln_g, qb=L0_attn_q_ln_b,
        wdkv=L0_attn_W_dkv, wukv=L0_attn_W_ukv, kg=L0_attn_kv_ln_g, kb=L0_attn_kv_ln_b, wo=L0_attn_W_o,
        taps=L0_xattn_ssm_kernel, skip=L0_xattn_D, gate=L0_ffn_gate_w, w13=L0_ffn_w13, w2=L0_ffn_w2,
        sw13=L0_ffn_sw13, sw2=L0_ffn_sw2).items()}

    def chunked(w):
        return np.ascontiguousarray(w.reshape(-1, P, w.shape[1]).transpose(1, 0, 2).reshape(P, -1))

    w_k = np.zeros((LAT, DC, 2, H // DC, DH), f)
    for v in range(2):
        w_k[:, :, v, v::2] = a["wukv"][:, 0:D].reshape(LAT, DC, H // DC, DH)[:, :, v::2]
    lat_up = np.zeros((P, 4 * D), f)
    lat_up[0:LAT, 0:D] = a["wuq"]
    lat_up[LAT:, D:2 * D] = a["wukv"][:, D:]
    lat_up[LAT:, 2 * D:] = w_k.reshape(LAT, 2 * D)
    padded = np.concatenate([np.zeros((HS, P - 1), f), a["taps"]], axis=1)
    toep = np.empty((HS, P, 2 * P + 1), f)
    toep[:, :, 0:2 * P] = padded[:, P - 1 - np.arange(P)[:, None] + np.arange(2 * P)[None, :]]
    toep[:, :, 2 * P] = a["skip"][:, None]
    ctx_t = a["ctx"].reshape(B, HS, HD, DC, P).transpose(1, 4, 3, 0, 2)
    ctx_t = np.concatenate([ctx_t, ctx_t[..., 0:HW - HD]], axis=4).reshape(HS, P, DC * B * HW)
    s13 = a["sw13"].reshape(2, NS, I, D).transpose(1, 0, 2, 3).reshape(NS, UC, D)
    w13 = np.concatenate([a["w13"], s13], axis=0)
    w_up = w13.reshape(NE, UC, DC, P).transpose(3, 2, 0, 1).reshape(P, NW_UP)
    w2 = np.concatenate([a["w2"].transpose(0, 2, 1).reshape(E * I, D), a["sw2"].T,
                         np.zeros((NCH * P - HCOLS, D), f)], axis=0)

    arrays = dict(
        x=a["x"], ctx_t=ctx_t, lat_down=chunked(np.concatenate([a["wdq"], a["wdkv"]], axis=1)),
        lat_gb=np.stack([np.concatenate([a["qg"], a["kg"]]), np.concatenate([a["qb"], a["kb"]])], axis=1),
        lat_up=lat_up, w_o=chunked(a["wo"].T), toep=toep, gate_w=chunked(a["gate"].T), w_up=w_up, w_dn=chunked(w2))
    nc = bacc.Bacc("TRN2", target_bir_lowering=False, num_devices=1)
    arrays = {f"in_{k}": np.ascontiguousarray(w) for k, w in arrays.items()}
    args = [nc.dram_tensor(k, w.shape, F32, kind="ExternalInput").ap() for k, w in arrays.items()]
    out = nc.dram_tensor("out_x", (B, S, D), F32, kind="ExternalOutput").ap()
    build(nc, *args, out)
    r = run_bass_kernel_spmd(nc, [arrays], core_ids=[0])
    return r.results[0]["out_x"]
```
